# Optimizing a Trainium2 kernel written in Bass

```python
import numpy as np
import jax
import jax.numpy as jnp

def _softmax(x, axis=-1):
    return jax.nn.softmax(x, axis=axis)

def _gelu(x):
    return jax.nn.gelu(x, approximate=True)

def _silu(x):
    return jax.nn.silu(x)

def _sigmoid(x):
    return jax.nn.sigmoid(x)

def _layernorm(x, axis=-1, eps=1e-05):
    m = jnp.mean(x, axis=axis, keepdims=True)
    v = jnp.var(x, axis=axis, keepdims=True)
    return (x - m) / jnp.sqrt(v + eps)

def _scatter_add(tgt, idx, src, axis=0):
    return tgt.at[idx].add(src)

def _segment_sum(src, seg, n):
    return jax.ops.segment_sum(src, seg, n)
kernel_name = 'mk_perceiver_d1_seqx_r4_10d737'

def setup_inputs(seed: int=0):
    np.random.seed(seed)
    _w = jnp.asarray

    def _rec_inputs():
        import jax
        import jax.numpy as jnp
        _rk = jax.random.key(seed)
        x = -0.0002928 + 1 * jax.random.normal(jax.random.fold_in(_rk, 1), (32, 64, 256), jnp.float32)
        _lenS = 64 - jax.random.randint(jax.random.fold_in(_rk, 7), (32,), 0, max(1, 64 // 4) + 1, jnp.int32)
        _lenS2 = 256 - jax.random.randint(jax.random.fold_in(_rk, 8), (32,), 0, max(1, 256 // 4) + 1, jnp.int32)
        _ctx_1024P = jax.random.normal(jax.random.fold_in(_rk, 11), (32, 16, 256), jnp.float32)
        _ctx_1024c = jax.random.dirichlet(jax.random.fold_in(_rk, 511), 0.3 * jnp.ones((16,), jnp.float32), (32, 256))
        _ctx_1024t = jnp.einsum('bsk,bkd->bsd', _ctx_1024c, _ctx_1024P)
        _ctx_1024t = _ctx_1024t * jax.lax.rsqrt(jnp.mean(jnp.square(_ctx_1024t)) + 1e-12) * 0.953939
        ctx_1024 = -1.39393e-06 + 0.999914 * (_ctx_1024t + 0.3 * jax.random.normal(jax.random.fold_in(_rk, 611), (32, 256, 256), jnp.float32))
        _validS = jnp.arange(64)[None, :] < _lenS[:, None]
        _validS2 = jnp.arange(256)[None, :] < _lenS2[:, None]
        _causal = jnp.tril(jnp.ones((64, 64), dtype=bool))
        mask_B_ik0 = jnp.where(jnp.ones((32,), dtype=bool), 68, 1563).astype(jnp.int32)
        return (x, ctx_1024, mask_B_ik0)
    x, ctx_1024, mask_B_ik0 = _rec_inputs()

    def _L0_xattn_setup():
        import jax, jax.numpy as jnp
        import numpy as np
        B, S, D, H = (2, 512, 256, 16)
        DH = D // H

        def _split_heads(x):
            b, s, _ = x.shape
            return x.reshape(b, s, H, DH).transpose(0, 2, 1, 3)
        key = jax.random.key(seed)
        k = jax.random.split(key, 8)
        scale = 0.02
        return {'queries': jax.random.normal(k[0], (B, S, D), dtype=jnp.float32), 'keys': jax.random.normal(k[1], (B, S, D), dtype=jnp.float32), 'values': jax.random.normal(k[2], (B, S, D), dtype=jnp.float32), 'valid_length': jax.random.randint(k[3], (B,), 0, S, dtype=jnp.int64), 'Wq': jax.random.normal(k[4], (D, D), dtype=jnp.float32) * scale, 'Wk': jax.random.normal(k[5], (D, D), dtype=jnp.float32) * scale, 'Wv': jax.random.normal(k[6], (D, D), dtype=jnp.float32) * scale, 'Wo': jax.random.normal(k[7], (D, D), dtype=jnp.float32) * scale}
    _L0_xattn_all = _L0_xattn_setup()
    _L0_xattn_in = {k: v for k, v in _L0_xattn_all.items() if k in ('Wq', 'Wk', 'Wv', 'Wo')}
    del _L0_xattn_all

    def _L0_attn_setup():
        import jax, jax.numpy as jnp
        import numpy as np
        D_MODEL = 256
        N_HEADS = 16
        D_HEAD = 64
        BATCH = 4
        SEQ = 512
        NEG = -1000000000.0
        key = jax.random.key(seed)
        k1, k2, k3, k4, k5 = jax.random.split(key, 5)
        x = jax.random.normal(k1, (BATCH, SEQ, D_MODEL), dtype=jnp.float32)
        std = 0.02
        wq = jax.random.normal(k2, (N_HEADS, D_HEAD, D_MODEL), dtype=jnp.float32) * std
        wk = jax.random.normal(k3, (N_HEADS, D_HEAD, D_MODEL), dtype=jnp.float32) * std
        wv = jax.random.normal(k4, (N_HEADS, D_HEAD, D_MODEL), dtype=jnp.float32) * std
        wo = jax.random.normal(k5, (D_MODEL, N_HEADS * D_HEAD), dtype=jnp.float32) * std
        return {'x': x, 'wq': wq, 'wk': wk, 'wv': wv, 'wo': wo}
    _L0_attn_all = _L0_attn_setup()
    _L0_attn_in = {k: v for k, v in _L0_attn_all.items() if k in ('wq', 'wk', 'wv', 'wo')}
    del _L0_attn_all

    def _L0_ffn_setup():
        import jax, jax.numpy as jnp
        import numpy as np

        def _ste(w, w_q):
            return w + jax.lax.stop_gradient(w_q - w)

        def quantize_w8_per(w, axis):
            amax = jnp.clip(jnp.max(jnp.abs(w), axis=axis, keepdims=True), 1e-08, None)
            scale = 127.0 / amax
            w_q = jnp.clip(jnp.round(w * scale), -128.0, 127.0) / scale
            return _ste(w, w_q)

        def quantize_a16(x):
            amax = jnp.clip(jnp.max(jnp.abs(x)), 1e-08, None)
            scale = 32767.0 / amax
            x_q = jnp.clip(jnp.round(x * scale), -32768.0, 32767.0) / scale
            return _ste(x, x_q)
        key = jax.random.key(seed)
        k1, k2, k3 = jax.random.split(key, 3)
        d_model, d_ff = (256, 1024)
        x = jax.random.normal(k1, (4, 512, d_model), dtype=jnp.float32)
        W_in = jax.random.normal(k2, (d_model, d_ff), dtype=jnp.float32) / np.sqrt(d_model)
        b_in = jnp.zeros((d_ff,), dtype=jnp.float32)
        W_out = jax.random.normal(k3, (d_ff, d_model), dtype=jnp.float32) / np.sqrt(d_ff)
        b_out = jnp.zeros((d_model,), dtype=jnp.float32)
        return {'x': x, 'W_in': W_in, 'b_in': b_in, 'W_out': W_out, 'b_out': b_out}
    _L0_ffn_all = _L0_ffn_setup()
    _L0_ffn_in = {k: v for k, v in _L0_ffn_all.items() if k in ('W_in', 'b_in', 'W_out', 'b_out')}
    del _L0_ffn_all
    return {'x': x, 'ctx_1024': ctx_1024, 'mask_B_ik0': mask_B_ik0, 'L0_xattn_Wq': _L0_xattn_in['Wq'], 'L0_xattn_Wk': _L0_xattn_in['Wk'], 'L0_xattn_Wv': _L0_xattn_in['Wv'], 'L0_xattn_Wo': _L0_xattn_in['Wo'], 'L0_attn_wq': _L0_attn_in['wq'], 'L0_attn_wk': _L0_attn_in['wk'], 'L0_attn_wv': _L0_attn_in['wv'], 'L0_attn_wo': _L0_attn_in['wo'], 'L0_ffn_W_in': _L0_ffn_in['W_in'], 'L0_ffn_b_in': _L0_ffn_in['b_in'], 'L0_ffn_W_out': _L0_ffn_in['W_out'], 'L0_ffn_b_out': _L0_ffn_in['b_out']}

def reference(x, ctx_1024, mask_B_ik0, L0_xattn_Wq, L0_xattn_Wk, L0_xattn_Wv, L0_xattn_Wo, L0_attn_wq, L0_attn_wk, L0_attn_wv, L0_attn_wo, L0_ffn_W_in, L0_ffn_b_in, L0_ffn_W_out, L0_ffn_b_out):
    import jax
    import jax.numpy as jnp

    def _L0_xattn_ref(queries, keys, values, valid_length, Wq, Wk, Wv, Wo):
        import jax, jax.numpy as jnp
        import numpy as np
        B, S, D, H = (2, 512, 256, 16)
        DH = D // H

        def _split_heads(x):
            b, s, _ = x.shape
            return x.reshape(b, s, H, DH).transpose(0, 2, 1, 3)
        q = _split_heads(queries @ Wq)
        k = _split_heads(keys @ Wk)
        v = _split_heads(values @ Wv)
        scores = jnp.einsum('bhqd,bhkd->bhqk', q, k)
        attn = jax.nn.softmax(scores, axis=-1)
        out = jnp.einsum('bhqk,bhkd->bhqd', attn, v)
        out = out.transpose(0, 2, 1, 3).reshape(queries.shape[0], queries.shape[1], D)
        return out @ Wo

    def _L0_attn_ref(x, wq, wk, wv, wo):
        import jax, jax.numpy as jnp
        import numpy as np
        D_MODEL = 256
        N_HEADS = 16
        D_HEAD = 64
        BATCH = 4
        SEQ = 512
        NEG = -1000000000.0
        b, s, _ = x.shape
        scale = jnp.sqrt(jnp.asarray(D_HEAD, x.dtype))
        q = jnp.einsum('bsd,hed->bhse', x, wq)
        k = jnp.einsum('bsd,hed->bhse', x, wk)
        v = jnp.einsum('bsd,hed->bhse', x, wv)
        scores = jnp.einsum('bhse,bhte->bhst', q, k) / scale
        causal_mask = jnp.triu(jnp.ones((s, s), dtype=bool), k=1)
        scores = jnp.where(causal_mask, jnp.asarray(NEG, scores.dtype), scores)
        weights = jax.nn.softmax(scores, axis=-1)
        heads = jnp.einsum('bhst,bhte->bhse', weights, v)
        concat = heads.transpose(0, 2, 1, 3).reshape(b, s, N_HEADS * D_HEAD)
        return concat @ wo.T

    def _L0_ffn_ref(x, W_in, b_in, W_out, b_out):
        import jax, jax.numpy as jnp
        import numpy as np

        def _ste(w, w_q):
            return w + jax.lax.stop_gradient(w_q - w)

        def quantize_w8_per(w, axis):
            amax = jnp.clip(jnp.max(jnp.abs(w), axis=axis, keepdims=True), 1e-08, None)
            scale = 127.0 / amax
            w_q = jnp.clip(jnp.round(w * scale), -128.0, 127.0) / scale
            return _ste(w, w_q)

        def quantize_a16(x):
            amax = jnp.clip(jnp.max(jnp.abs(x)), 1e-08, None)
            scale = 32767.0 / amax
            x_q = jnp.clip(jnp.round(x * scale), -32768.0, 32767.0) / scale
            return _ste(x, x_q)
        W_in_sim = quantize_w8_per(W_in, axis=0)
        W_out_sim = quantize_w8_per(W_out, axis=1)
        x_sim = quantize_a16(x)
        hidden = jax.nn.gelu(x_sim @ W_in_sim + b_in, approximate=False)
        hidden_sim = quantize_a16(hidden)
        out = hidden_sim @ W_out_sim + b_out
        return out
    x = x + _L0_xattn_ref(_layernorm(x, axis=-1), ctx_1024, ctx_1024, mask_B_ik0, L0_xattn_Wq, L0_xattn_Wk, L0_xattn_Wv, L0_xattn_Wo)
    x = x + _L0_attn_ref(_layernorm(x, axis=-1), L0_attn_wq, L0_attn_wk, L0_attn_wv, L0_attn_wo)
    x = x + _L0_ffn_ref(_layernorm(x, axis=-1), L0_ffn_W_in, L0_ffn_b_in, L0_ffn_W_out, L0_ffn_b_out)
    return x

_drawn_inputs = setup_inputs


def setup_inputs(seed=0):
    import zlib

    import numpy as np

    out = dict(_drawn_inputs(seed))
    spreads = {'L0_ffn_b_in': (0.0, 0.1), 'L0_ffn_b_out': (0.0, 0.1)}
    factors = {'L0_xattn_Wq': 7.068, 'L0_xattn_Wk': 7.052, 'L0_attn_wq': 8.0, 'L0_attn_wk': 8.0}
    for name, (base, spread) in spreads.items():
        noise = np.random.default_rng([zlib.crc32(name.encode()), seed]).standard_normal(out[name].shape)
        drawn = base * np.exp(spread * noise) if base else spread * noise
        out[name] = jnp.asarray(drawn.astype(out[name].dtype))
    for name, factor in factors.items():
        out[name] = (out[name] * factor).astype(out[name].dtype)
    return out
```

```python
from contextlib import ExitStack

import concourse.bass as bass
from concourse import mybir

ALU = mybir.AluOpType
ACT = mybir.ActivationFunctionType
AX = mybir.AxisListType
F32 = mybir.dt.float32
F32R = mybir.dt.float32r
F16 = mybir.dt.float16
BF16 = mybir.dt.bfloat16
RMAX = bass.bass_isa.ReduceOp.max

P = 128
B, SQ, D, SK = 32, 64, 256, 256
H = 16
XE = D // H
E = 64
HE = H * E
FF = 1024
TOK = B * SQ
TILES = TOK // P
QUADS = TILES // 2
KC = D // P
HP = H // 2
HI, LO = 0, 1
CONSTS = 13
LN_EPS = 1e-5
MASKED = -1e9 * 8.0
ROUND = 1.5 * 2.0 ** 23


def after(eng, sem, n):
    if isinstance(n, int) and n <= 0:
        return
    eng.wait_ge(sem, n)


def apart(eng, waited):
    eng.sem_inc(waited, 1)


def f32(ap):
    return ap.bitcast(F32)


def split_matmul(pe, out, w, x):
    n = len(w)
    for k in range(n):
        (wh, wl), (xh, xl) = w[k], x[k]
        pe.matmul(out, wh, xh, start=(k == 0), stop=False)
        pe.matmul(out, wh, xl, start=False, stop=False)
        last = pe.matmul(out, wl, xh, start=False, stop=(k == n - 1))
    return last


def build(nc, x, ctxT, xwq, xwk, xwv, xwo, awq, awk, awv, awo, w_inT, b_in, w_out, b_out, out):
    with ExitStack() as whole:
        def keep(name, shape, dt):
            return whole.enter_context(nc.sbuf_tensor(name, shape, dt))

        X = keep("X", [P, TILES, D], F32)
        ident = keep("ident", [P, P], F32)
        identb = keep("identb", [P, P], BF16)
        fold = keep("fold", [P, SQ], F32)
        parity = keep("parity", [P, 2], F32)
        causal = keep("causal", [P, HP, SQ], BF16)
        half = keep("half", [P, 2], F32)
        cross_attention(nc, X, ident, identb, fold, parity, causal, half, x, ctxT, xwq, xwk, xwv, xwo)
        self_attention(nc, X, ident, identb, causal, half, awq, awk, awv, awo)
        feed_forward(nc, X, ident, identb, w_inT, b_in, w_out, b_out, out)


def constants(pool, consts, ident, identb, fold, parity, causal, half):
    made = 0

    def in_turn(instruction):
        nonlocal made
        made += 1
        instruction.then_inc(consts, 1)
        pool.wait_ge(consts, made)

    in_turn(pool.memset(ident[:, :], 0.0))
    in_turn(pool.affine_select(out=ident[:, :], in_=ident[:, :], compare_op=ALU.not_equal, fill=1.0,
                               base=0, pattern=[[-1, P]], channel_multiplier=1))
    in_turn(pool.tensor_copy(identb[:, :], ident[:, :]))
    in_turn(pool.memset(half[:, :], -0.5))
    in_turn(pool.memset(fold[:, :], 0.0))
    in_turn(pool.memset(parity[:, :], 0.0))
    in_turn(pool.memset(causal[:, :, :], 0.0))
    for s in range(2):
        rows = slice(64 * s, 64 * s + 64)
        in_turn(pool.affine_select(out=fold[rows, :], in_=fold[rows, :], compare_op=ALU.not_equal, fill=1.0,
                                   base=0, pattern=[[-1, SQ]], channel_multiplier=1))
        in_turn(pool.memset(parity[rows, s:s + 1], 1.0))
        in_turn(pool.affine_select(out=causal[rows], in_=causal[rows], compare_op=ALU.is_ge, fill=MASKED,
                                   base=0, pattern=[[0, HP], [-1, SQ]], channel_multiplier=1))
    assert made == CONSTS


def cross_attention(nc, X, ident, identb, fold, parity, causal, half, x, ctxT, xwq, xwk, xwv, xwo):
    CK = SK
    PK = 2 * CK
    KT = CK // P
    CHUNKS = 8
    PAIRS = TILES
    EV = 10
    EV0 = 8
    RESTACK = 12 * 16
    with ExitStack() as ctx:
        def sb(name, shape, dt):
            return ctx.enter_context(nc.sbuf_tensor(name, shape, dt))

        def ps(name, shape):
            return ctx.enter_context(nc.psum_tensor(name, shape, F32))

        def sem(name):
            return ctx.enter_context(nc.semaphore("x_" + name))

        wraw = sb("wraw", [P, 4, KC, D], F32)
        W = [sb(f"W{s}", [P, 4, KC, D], F32R) for s in "hl"]
        CT = [sb(f"CT{i}", [P, KC, PK], F32) for i in range(2)]
        CS = [sb(f"CS{s}", [P, KC, PK], F32R) for s in "hl"]
        stats = sb("stats", [P, 2, 6], F32)
        mv = sb("mv", [P, 2, 2], F32)
        vare = sb("vare", [P, 2], F32)
        rstd = sb("rstd", [P, 2], F32)
        XN = sb("XN", [P, 2, D], F32)
        XT = [sb(f"XT{s}", [P, KC, 2 * P], F32R) for s in "hl"]
        QS = [sb(f"QS{s}", [P, 2, 2, 2, SQ], F32R) for s in "hl"]
        KS = [sb(f"KS{s}", [P, 2, PK], F32R) for s in "hl"]
        Kst = [sb(f"Kst{i}", [96, HP, PK], F32R) for i in range(2)]
        Qraw = sb("Qraw", [96, 4, 2, 2, 2, SQ], F32)
        rows_of = sb("rows_of", [96, 2], F32)
        Qst = [sb(f"Qst{i}", [96, 4, 2, 2, 2, SQ], F32R) for i in range(2)]
        V = [sb(f"V{i}", [P, 2 * KT, HP, 3, 2 * XE], BF16) for i in range(2)]
        VR = [sb(f"VR{i}", [P, 2, D], F32) for i in range(2)]
        nmax = [sb(f"nmax{i}", [P, 2], F32) for i in range(2)]
        Pr = [sb(f"Pr{i}", [P, 2, CK], F32) for i in range(2)]
        Ph = [sb(f"Ph{i}", [P, 2, KT, P], F16) for i in range(2)]
        Pl = [sb(f"Pl{i}", [P, 2, KT, P], F16) for i in range(2)]
        rsum = [sb(f"rsum{i}", [P, 4], F32) for i in range(4)]
        rinv = sb("rinv", [P, 4], F32)
        rmask = sb("rmask", [P, 4, 2], F32)
        Osum = sb("Osum", [P, 4, 2 * XE], F32)
        On = sb("On", [P, 4, 2 * XE], F32)
        OT = [sb(f"OT{s}", [P, 2, P], F32R) for s in "hl"]

        pS = [ps(f"pS{i}", [P, 2, CK]) for i in range(2)]
        pT = [ps(f"pT{i}", [P, 2, KT, P]) for i in range(2)]
        pJ = [ps(f"pJ{i}", [P, 512]) for i in range(2)]
        pO = ps("pO", [P, 4, 3, 2 * XE])
        pM = ps("pM", [P, 512])
        pOT = pM[:, 0:256].rearrange("p (g t) -> p g t", g=2)
        pY = pM[:, 256:512]

        x_in0, x_in, w_in = sem("x_in0"), sem("x_in"), sem("w_in")
        w_hi, w_lo = sem("w_hi"), sem("w_lo")
        ctx_in = [sem(f"ctx_in{i}") for i in range(2)]
        ctx_hi, ctx_lo = sem("ctx_hi"), sem("ctx_lo")
        consts = sem("consts")
        waited = sem("waited")
        ln_st, ln_mv, ln_ve, ln_rs, ln_xn = sem("ln_st"), sem("ln_mv"), sem("ln_ve"), sem("ln_rs"), sem("ln_xn")
        proj, hi, lo = sem("proj"), sem("hi"), sem("lo")
        v2_done, v3_done = sem("v2"), sem("v3")
        kst_in = [sem(f"kst_in{i}") for i in range(2)]
        qraw_in, q_taken, q_half, rows_made = sem("qraw_in"), sem("q_taken"), sem("q_half"), sem("rows_made")
        scores, maxed, exped, turned = sem("scores"), sem("maxed"), sem("exped"), sem("turned")
        ph_done, pl_done, pv_done = sem("ph"), sem("pl"), sem("pv")
        rinv_done, rmask_done, osum_done, on_done = sem("rinv"), sem("rmask"), sem("osum"), sem("on")
        folded, oth, otl, y_done, x_done = sem("folded"), sem("oth"), sem("otl"), sem("y"), sem("x")

        AHEAD = [("X", 0, 0), ("K", 0, 0), ("K", 0, 1), ("Q", 0, 0), ("V", 0, 0), ("V", 0, 1), ("K", 1, 0), ("K", 1, 1)]
        EVENTS = {1: (0, "V", 1, 0), 2: (1, "V", 1, 1), 4: (2, "X", 2, 0), 5: (3, "Q", 2, 0), 6: (4, "K", 2, 0),
                  7: (5, "K", 2, 1), 9: (6, "V", 2, 0), 10: (7, "V", 2, 1), 14: (8, "K", 3, 0), 15: (9, "K", 3, 1)}

        def event(i, c, last):
            if c not in EVENTS:
                return None
            k, kind, ahead, part = EVENTS[c]
            if last and k >= 2:
                return None
            return EV0 + EV * i + k, k, kind, ahead, part

        def steps(eng, body):
            body(0, False)
            with eng.Fori(1, QUADS - 1) as i:
                body(i, False)
            body(QUADS - 1, True)

        block = ctx.enter_context(nc.Block())

        @block.sync
        def _(sp):
            for n in range(4):
                sp.dma_start(X[:, 4 * n:4 * n + 4, :],
                             x[4 * P * n:4 * P * (n + 1), :].rearrange("(t p) d -> p t d", p=P)
                             ).then_inc(x_in if n else x_in0, 16)
                if n == 0:
                    for m, w in enumerate((xwq, xwk, xwv, xwo)):
                        sp.dma_start(wraw[:, m], w.rearrange("(k p) n -> p k n", p=P)).then_inc(w_in, 16)

            def load_ctx(pair, b, before):
                after(sp, ctx_hi, before)
                after(sp, ctx_lo, before)
                sp.dma_start(CT[b][:, :, :],
                             ctxT.rearrange("(k p) n -> p k n", p=P)[:, :, bass.ds(pair * PK, PK)]).then_inc(ctx_in[b], 16)

            def restack_k(b, r, chunks_done):
                after(sp, lo, r + 1)
                apart(sp, waited)
                after(sp, scores, chunks_done)
                for jj in range(4):
                    for u, part in enumerate((HI, HI, LO)):
                        sp.dma_start(f32(Kst[b][32 * u:32 * u + 32, jj:HP:4, :]),
                                     f32(KS[part][32 * jj:32 * jj + 32, :, :])).then_inc(kst_in[b], 16)

            def restack_q(r, quads_taken):
                after(sp, lo, r + 1)
                apart(sp, waited)
                after(sp, q_taken, 2 * quads_taken)
                for jj in range(4):
                    for u, part in enumerate((HI, LO, HI)):
                        sp.dma_start(Qraw[32 * u:32 * u + 32, jj],
                                     f32(QS[part][32 * jj:32 * jj + 32])).then_inc(qraw_in, 16)

            load_ctx(0, 0, 0)
            load_ctx(1, 1, 0)
            restack_k(0, 2, 0)
            restack_q(3, 0)
            restack_k(1, 7, 0)

            def body(i, last):
                p = 2 * i
                if not last:
                    load_ctx(p + 2, 0, p + 1)
                    load_ctx(p + 3, 1, p + 2)
                    restack_q(EV0 + EV * i + 3, i + 1)
                    restack_k(0, EV0 + EV * i + 5, CHUNKS * (p + 1))
                    restack_k(1, EV0 + EV * i + 9, CHUNKS * (p + 2))

            steps(sp, body)

        @block.gpsimd
        def _(pool):
            constants(pool, consts, ident, identb, fold, parity, causal, half)

            def rstd_of(n):
                pool.wait_ge(ln_mv, 2 * n + 2)
                apart(pool, waited)
                pool.tensor_scalar(vare[:, :], mv[:, :, 1], LN_EPS, None, ALU.add).then_inc(ln_ve, 1)
                pool.wait_ge(ln_ve, n + 1)
                pool.tensor_tensor(rstd[:, :], vare[:, :], half[:, :], ALU.pow).then_inc(ln_rs, 1)

            def ctx_low(b, n):
                pool.wait_ge(ctx_hi, n)
                pool.tensor_tensor(CS[LO][:, :, :], CT[b][:, :, :], f32(CS[HI][:, :, :]), ALU.subtract).then_inc(ctx_lo, 1)

            def v3(b, part, n):
                pool.wait_ge(v2_done, n)
                pool.tensor_tensor(V[b][:, 2 * part:2 * part + 2, :, 2, :],
                                   VR[part][:, :, :].rearrange("p t (j c) -> p t j c", j=HP),
                                   V[b][:, 2 * part:2 * part + 2, :, 1, :], ALU.subtract).then_inc(v3_done, 1)

            def take_q(r, quad, chunks_done):
                pool.wait_ge(qraw_in, RESTACK * (quad + 1))
                after(pool, scores, chunks_done)
                for h2 in range(2):
                    last = pool.tensor_tensor(
                        Qst[r][:, :, :, :, h2, :].rearrange("p j g a q -> p (j g a) q"),
                        Qraw[:, :, r].rearrange("p j g a q -> p j (g a) q"),
                        rows_of[:, h2:h2 + 1].unsqueeze(2).unsqueeze(3).to_broadcast([96, 4, 4, SQ]), ALU.mult)
                    if h2 == 0:
                        last.then_inc(q_half, 1)
                last.then_inc(q_taken, 1)

            rstd_of(0)
            ctx_low(0, 1)
            for u in range(3):
                rows = rows_of[32 * u:32 * u + 32, :]
                pool.memset(rows, 1.0).then_inc(rows_made, 1)
                pool.wait_ge(rows_made, 3 * u + 1)
                pool.affine_select(out=rows, in_=rows, compare_op=ALU.is_ge, fill=0.0,
                                   base=0, pattern=[[-XE, 2]], channel_multiplier=1).then_inc(rows_made, 1)
                pool.wait_ge(rows_made, 3 * u + 2)
                pool.affine_select(out=rows, in_=rows, compare_op=ALU.is_ge, fill=0.0,
                                   base=XE - 1, pattern=[[XE, 2]], channel_multiplier=-1).then_inc(rows_made, 1)
                pool.wait_ge(rows_made, 3 * u + 3)
            take_q(0, 0, 0)
            v3(0, 0, 1)
            v3(0, 1, 2)
            ctx_low(1, 2)
            take_q(1, 0, 0)

            def body(i, last):
                if not (isinstance(i, int) and i == 0):
                    take_q(1, i, CHUNKS * 2 * i)
                if not last:
                    rstd_of(i + 1)
                v3(1, 0, 4 * i + 3)
                v3(1, 1, 4 * i + 4)
                if not last:
                    ctx_low(0, 2 * i + 3)
                    take_q(0, i + 1, CHUNKS * (2 * i + 1))
                    v3(0, 0, 4 * i + 5)
                    v3(0, 1, 4 * i + 6)
                    ctx_low(1, 2 * i + 4)

            steps(pool, body)

        @block.tensor
        def _(pe):
            def parts(ts, cols=slice(None)):
                return [(ts[HI][:, k, cols], ts[LO][:, k, cols]) for k in range(KC)]

            def weights(m, cols=slice(None)):
                return [(W[HI][:, m, k, cols], W[LO][:, m, k, cols]) for k in range(KC)]

            def project(r, k_, kind, part, pair, q_needs=None):
                after(pe, lo, r - 1)
                bank = pJ[k_ % 2]
                if kind == "X":
                    pe.wait_ge(ln_xn, pair + 2)
                    for k in range(KC):
                        for t in range(2):
                            last = pe.transpose(bank[:, 256 * k + P * t:256 * k + P * t + P],
                                                XN[:, t, P * k:P * k + P], ident[:, :])
                elif kind == "Q":
                    pe.wait_ge(lo, q_needs)
                    for g in range(2):
                        last = split_matmul(pe, bank[:, 256 * g:256 * g + 256], weights(0, slice(P * g, P * g + P)),
                                            parts(XT))
                elif kind == "K":
                    pe.wait_ge(ctx_lo, pair + 1)
                    last = split_matmul(pe, bank[:, :], weights(1, slice(P * part, P * part + P)), parts(CS))
                else:
                    for t in range(2):
                        keys = slice(P * (2 * part + t), P * (2 * part + t) + P)
                        last = split_matmul(pe, bank[:, 256 * t:256 * t + 256], parts(CS, keys), weights(2))
                last.then_inc(proj, 1)

            def score(i, s):
                par, c = s // 8 % 2, s % 8
                b, jj = c // 4, c % 4
                if c == 0:
                    pe.wait_ge(kst_in[par], RESTACK * (i + 1 + s // 16))
                    pe.wait_ge(q_taken, 2 * i + s // 8 + 1)
                after(pe, exped, 2 * (16 * i + s) - 2)
                for t in range(2):
                    j = 2 * jj + t
                    last = pe.matmul(pS[c % 2][:, t, :], Qst[par][:, j % 4, j // 4, b, :, :],
                                     Kst[par][:, j, CK * b:CK * b + CK], start=True, stop=True)
                last.then_inc(scores, 1)

            def turn(i, s):
                pe.wait_ge(exped, 2 * (16 * i + s) + 2)
                after(pe, pl_done, 16 * i + s - 1)
                for t in range(2):
                    for k in range(KT):
                        last = pe.transpose(pT[s % 2][:, t, k, :], Pr[s % 2][:, t, P * k:P * k + P], ident[:, :])
                last.then_inc(turned, 1)

            def weigh(i, s):
                par, c = s // 8 % 2, s % 8
                b, jj = c // 4, c % 4
                pe.wait_ge(pl_done, 16 * i + s + 1)
                if c == 0:
                    pe.wait_ge(v3_done, 4 * i + 2 + 2 * (s // 8))
                if c % 2 == 0:
                    after(pe, osum_done, 8 * i + s // 2)
                for t in range(2):
                    j = 2 * jj + t
                    for k in range(KT):
                        v = V[par][:, KT * b + k, j, :, :]
                        pe.matmul(pO[:, j % 4, :, :], Ph[c % 2][:, t, k, :], v, start=(k == 0), stop=False,
                                  skip_group_check=True)
                        last = pe.matmul(pO[:, j % 4, 0:2, :], Pl[c % 2][:, t, k, :], v[:, 0:2, :], start=False,
                                         stop=(k == KT - 1), skip_group_check=True)
                last.then_inc(pv_done, 1)

            def fold_heads(i, h):
                b, g = h // 2 % 2, h % 2
                pe.wait_ge(on_done, 8 * i + h + 1)
                if h % 4 == 0:
                    after(pe, otl, 2 * i + h // 4)
                if h % 4 == 1:
                    after(pe, x_done, 2 * i + h // 4)
                pe.matmul(pOT[:, g, SQ * b:SQ * b + SQ], On[:, :, :], fold[:, :], start=True, stop=True
                          ).then_inc(folded, 1)

            def project_out(pair):
                pe.wait_ge(otl, pair + 1)
                after(pe, x_done, pair)
                split_matmul(pe, pY, parts(OT), weights(3)).then_inc(y_done, 1)

            pe.wait_ge(consts, CONSTS)
            pe.wait_ge(w_lo, 4)
            for r, (kind, ahead, part) in enumerate(AHEAD):
                if r == 6:
                    score(0, 0)
                    score(0, 1)
                project(r, r, kind, part, ahead, 1)

            def body(i, last):
                first = isinstance(i, int) and i == 0
                for s in range(16):
                    turn(i, s)
                    if not (last and s >= 14):
                        score(i, s + 2)
                    if event(i, s, last):
                        r, k, kind, ahead, part = event(i, s, last)
                        project(r, k, kind, part, 2 * i + ahead, r)
                    if not (first and s == 0):
                        weigh(i, s - 1)
                    if s % 2 == 0 and not (first and s < 4):
                        fold_heads(i, s // 2 - 2)
                    if s == 12 or (s == 4 and not first):
                        project_out(2 * i + (s - 12) // 8)

            steps(pe, body)
            weigh(QUADS - 1, 15)
            fold_heads(QUADS - 1, 6)
            fold_heads(QUADS - 1, 7)
            project_out(PAIRS - 1)

        def target(s_, kind, part):
            if kind == "X":
                return XT[s_][:, :, :], "p (k n) -> p k n", dict(k=KC)
            if kind == "Q":
                return (QS[s_][:, :, :, :, :].rearrange("p r g a q -> p g r (a q)"), "p (g r n) -> p g r n",
                        dict(g=2, r=2))
            return KS[s_][:, part, :], "p n -> p n", {}

        def reused(eng, i, kind, ahead):
            if i is None:
                if kind == "K" and ahead == 1:
                    eng.wait_ge(kst_in[0], RESTACK)
                return
            if kind == "K":
                eng.wait_ge(kst_in[(ahead - 1) % 2], RESTACK * (i + (ahead + 1) // 2))
            elif kind == "Q":
                eng.wait_ge(qraw_in, RESTACK * (i + 1))
            elif kind == "V":
                after(eng, pv_done, CHUNKS * (2 * i + ahead - 1))

        @block.scalar
        def _(act):
            def high(r, k, kind, ahead, part, i):
                act.wait_ge(proj, r + 1)
                reused(act, i, kind, ahead)
                bank = pJ[k % 2]
                if kind == "V":
                    act.activation(V[ahead % 2][:, 2 * part:2 * part + 2, :, 0, :],
                                   bank[:, :].rearrange("p (t j c) -> p t j c", t=2, j=HP), ACT.Copy).then_inc(hi, 1)
                else:
                    dst, how, kw = target(HI, kind, part)
                    act.activation(dst, bank[:, :].rearrange(how, **kw) if kw else bank[:, :], ACT.Copy).then_inc(hi, 1)

            def ctx_high(b, loads, proj_done):
                act.wait_ge(ctx_in[b], 16 * loads)
                after(act, proj, proj_done)
                act.activation(CS[HI][:, :, :], CT[b][:, :, :], ACT.Copy).then_inc(ctx_hi, 1)

            def exps(i, s):
                c = s % 8
                act.wait_ge(maxed, 16 * i + s + 1)
                after(act, turned, 16 * i + s - 1)
                for t in range(2):
                    q = 2 * (c % 2) + t
                    act.activation(Pr[c % 2][:, t, :], pS[c % 2][:, t, :], ACT.Exp, bias=nmax[c % 2][:, t:t + 1],
                                   accum_out=rsum[s // 2 % 4][:, q:q + 1]).then_inc(exped, 1)

            def p_high(i, s):
                act.wait_ge(turned, 16 * i + s + 1)
                after(act, pv_done, 16 * i + s - 1)
                act.activation(Ph[s % 2][:, :, :, :], pT[s % 2][:, :, :, :], ACT.Copy).then_inc(ph_done, 1)

            def o_high(pair):
                act.wait_ge(folded, 4 * pair + 4)
                after(act, y_done, pair)
                act.activation(OT[HI][:, :, :], pOT, ACT.Copy).then_inc(oth, 1)

            act.wait_ge(w_in, 64)
            for m in range(4):
                act.activation(W[HI][:, m], wraw[:, m], ACT.Copy).then_inc(w_hi, 1)
            ctx_high(0, 1, 0)
            for r, (kind, ahead, part) in enumerate(AHEAD):
                if r == 6:
                    ctx_high(1, 1, 6)
                    exps(0, 0)
                high(r, r, kind, ahead, part, None)

            def body(i, last):
                first = isinstance(i, int) and i == 0
                for s in range(16):
                    p_high(i, s)
                    if event(i, s, last):
                        r, k, kind, ahead, part = event(i, s, last)
                        high(r, k, kind, ahead, part, i)
                    if not (last and s == 15):
                        exps(i, s + 1)
                    if s == 11 or (s == 3 and not first):
                        o_high(2 * i + (s - 11) // 8)
                    if s == 3 and not last:
                        ctx_high(0, i + 2, EV0 + EV * i + 2)
                    if s == 11 and not last:
                        ctx_high(1, i + 2, EV0 + EV * i + 8)

            steps(act, body)
            o_high(PAIRS - 1)

        @block.vector
        def _(dve):
            def low(r, k, kind, ahead, part, i):
                dve.wait_ge(hi, r + 1)
                reused(dve, i, kind, ahead)
                bank = pJ[k % 2]
                if kind == "V":
                    v_no = 2 * ahead + part if i is None else 4 * i + 2 * ahead + part
                    after(dve, v3_done, v_no - 1)
                    rest = VR[part][:, :, :].rearrange("p t (j c) -> p t j c", j=HP)
                    tiles = V[ahead % 2][:, 2 * part:2 * part + 2]
                    dve.tensor_tensor(rest, bank[:, :].rearrange("p (t j c) -> p t j c", t=2, j=HP),
                                      tiles[:, :, :, 0, :], ALU.subtract).then_inc(lo, 1)
                    dve.wait_ge(lo, r + 1)
                    dve.tensor_copy(tiles[:, :, :, 1, :], rest).then_inc(v2_done, 1)
                else:
                    dst, how, kw = target(LO, kind, part)
                    high = f32(target(HI, kind, part)[0])
                    dve.tensor_tensor(dst, bank[:, :].rearrange(how, **kw) if kw else bank[:, :], high,
                                      ALU.subtract).then_inc(lo, 1)

            def statistics(i, quad):
                for t in range(2):
                    dve.bn_stats(stats[:, t, :], X[:, bass.ds(2 * quad + t, 1), :].rearrange("p a d -> p (a d)")
                                 ).then_inc(ln_st, 1)
                for t in range(2):
                    dve.wait_ge(ln_st, 2 * quad + t + 1)
                    apart(dve, waited)
                    dve.bn_aggr(mv[:, t, :], stats[:, t, :]).then_inc(ln_mv, 1)

            def normalize(quad):
                dve.wait_ge(ln_rs, quad + 1)
                for t in range(2):
                    dve.tensor_scalar(XN[:, t, :], X[:, bass.ds(2 * quad + t, 1), :].rearrange("p a d -> p (a d)"),
                                      mv[:, t, 0:1], rstd[:, t:t + 1], ALU.subtract, ALU.mult).then_inc(ln_xn, 1)

            def row_max(i, s):
                dve.wait_ge(scores, 16 * i + s + 1)
                dve.tensor_reduce(nmax[s % 2][:, :], pS[s % 2][:, :, :], AX.X, ALU.max, negate=True).then_inc(maxed, 1)

            def p_low(i, s):
                dve.wait_ge(ph_done, 16 * i + s + 1)
                dve.tensor_tensor(Pl[s % 2][:, :, :, :], pT[s % 2][:, :, :, :], Ph[s % 2][:, :, :, :], ALU.subtract
                                  ).then_inc(pl_done, 1)

            def norm(i, h):
                n = 8 * i + h
                dve.wait_ge(exped, 4 * n + 4)
                dve.reciprocal(rinv[:, :], rsum[h % 4][:, :]).then_inc(rinv_done, 1)
                dve.wait_ge(rinv_done, n + 1)
                dve.tensor_tensor(rmask[:, :, :], rinv[:, :].unsqueeze(2).to_broadcast([P, 4, 2]),
                                  parity[:, :].unsqueeze(1).to_broadcast([P, 4, 2]), ALU.mult).then_inc(rmask_done, 1)
                dve.wait_ge(pv_done, 2 * n + 2)
                dve.tensor_reduce(Osum[:, :, :], pO[:, :, :, :].rearrange("p j a c -> p j c a"), AX.X, ALU.add
                                  ).then_inc(osum_done, 1)
                dve.wait_ge(osum_done, n + 1)
                dve.wait_ge(rmask_done, n + 1)
                after(dve, folded, n)
                dve.tensor_tensor(On[:, :, :].rearrange("p j (a c) -> p j a c", a=2),
                                  Osum[:, :, :].rearrange("p j (a c) -> p j a c", a=2),
                                  rmask[:, :, :].unsqueeze(3).to_broadcast([P, 4, 2, XE]), ALU.mult).then_inc(on_done, 1)

            def o_low(pair):
                dve.wait_ge(oth, pair + 1)
                dve.tensor_tensor(OT[LO][:, :, :], pOT, f32(OT[HI][:, :, :]), ALU.subtract).then_inc(otl, 1)

            def add_rows(pair):
                dve.wait_ge(y_done, pair + 1)
                rows = X[:, bass.ds(pair, 1), :].rearrange("p a d -> p (a d)")
                dve.tensor_tensor(rows, pY, rows, ALU.add).then_inc(x_done, 1)

            dve.wait_ge(x_in0, 16)
            statistics(0, 0)
            normalize(0)
            for m in range(4):
                dve.wait_ge(w_hi, m + 1)
                dve.tensor_tensor(W[LO][:, m], wraw[:, m], f32(W[HI][:, m]), ALU.subtract).then_inc(w_lo, 1)
            for r, (kind, ahead, part) in enumerate(AHEAD):
                if r == 6:
                    row_max(0, 0)
                    row_max(0, 1)
                low(r, r, kind, ahead, part, None)
            dve.wait_ge(x_in, 48)

            def body(i, last):
                first = isinstance(i, int) and i == 0
                for s in range(16):
                    if s % 2 == 1 and not (first and s == 1):
                        norm(i, (s - 3) // 2)
                    p_low(i, s)
                    if event(i, s, last):
                        r, k, kind, ahead, part = event(i, s, last)
                        low(r, k, kind, ahead, part, i)
                    if not (last and s >= 14):
                        row_max(i, s + 2)
                    if s == 0 and not last:
                        statistics(i, i + 1)
                    if s == 2 and not last:
                        normalize(i + 1)
                    if s == 11 or (s == 3 and not first):
                        o_low(2 * i + (s - 11) // 8)
                    if s == 13 or (s == 5 and not first):
                        add_rows(2 * i + (s - 13) // 8)

            steps(dve, body)
            norm(QUADS - 1, 7)
            o_low(PAIRS - 1)
            add_rows(PAIRS - 1)


def self_attention(nc, X, ident, identb, causal, half, awq, awk, awv, awo):
    EV = 16
    EV0 = 14
    COPIES = 6
    QKV = [("Q", 0), ("Q", 1), ("Q", 2), ("Q", 3), ("K", 0), ("K", 1), ("K", 2), ("K", 3)]
    AHEAD = [("X", 0), ("X", 1)] + QKV + [("V", 0), ("V", 1), ("V", 2), ("V", 3)]
    BLOCK = 4 * 2 * SQ
    with ExitStack() as ctx:
        def sb(name, shape, dt):
            return ctx.enter_context(nc.sbuf_tensor("a_" + name, shape, dt))

        def ps(name, shape):
            return ctx.enter_context(nc.psum_tensor("a_" + name, shape, F32))

        def sem(name):
            return ctx.enter_context(nc.semaphore("a_" + name))

        raw = [sb(f"raw{i}", [P, KC, HE], F32) for i in range(4)]
        W = [[sb(f"W{m}{s}", [P, KC, HE], F32R) for s in "hl"] for m in range(3)]
        WO = [sb(f"WO{s}", [P, HP, D], F32R) for s in "hl"]
        stats = sb("stats", [P, 2, 6], F32)
        mv = sb("mv", [P, 2, 2], F32)
        vare = sb("vare", [P, 2], F32)
        rstd = sb("rstd", [P, 2], F32)
        XN = sb("XN", [P, 2, D], F32)
        XT = [sb(f"XT{s}", [P, KC, 2 * P], F32R) for s in "hl"]
        QT = sb("QT", [P, HP, 2 * P], F32)
        KT = sb("KT", [P, HP, 2 * P], F32)
        V = sb("V", [P, 2, HE], F32)
        rmax = sb("rmax", [P, 8], F32)
        Pr = [sb(f"Pr{s}", [P, 4, 2, SQ], F32) for s in range(4)]
        rsum = [sb(f"rsum{s}", [P, 8], F32) for s in range(4)]
        rinv = [sb(f"rinv{s}", [P, 8], F32) for s in range(4)]
        PT = [sb(f"PT{s}", [P, 4, P], F32) for s in range(2)]
        OT = [[sb(f"OT{t}{s}", [P, HP, P], F32R) for s in "hl"] for t in range(2)]

        pS = [ps(f"pS{s}", [P, BLOCK]) for s in range(4)]
        pJ = [ps(f"pJ{s}", [P, 512]) for s in range(2)]
        pO = [ps(f"pO{s}", [P, 4, P]) for s in range(2)]

        raw_in = [sem(f"raw_in{m}") for m in range(4)]
        w_hi, w_lo = sem("w_hi"), sem("w_lo")
        waited = sem("waited")
        ln_st, ln_mv, ln_ve, ln_rs, ln_xn = sem("ln_st"), sem("ln_mv"), sem("ln_ve"), sem("ln_rs"), sem("ln_xn")
        proj, xt_hi, xt_lo = sem("proj"), sem("xt_hi"), sem("xt_lo")
        by_act, by_dve = sem("by_act"), sem("by_dve")
        scored, maxed, shifted, exped, summed, inverted, weighted = (
            sem("scored"), sem("maxed"), sem("shifted"), sem("exped"), sem("summed"), sem("inverted"), sem("weighted"))
        turned, pt_done, pv_done, o_hi, o_lo, x_done = (
            sem("turned"), sem("pt"), sem("pv"), sem("o_hi"), sem("o_lo"), sem("x"))

        def o_half(s, b):
            bank = pS[s][:, :].rearrange("p (j n) -> p j n", j=4) if b else pO[s % 2][:, :, :]
            return bank[:, :, SQ * b:SQ * b + SQ]

        PLAN = ([("score", s) for s in range(4)]
                + [("X", 0, 0), ("X", 1, 1)] + [(kind, part, 2 + n) for n, (kind, part) in enumerate(QKV)]
                + [("turn", 0), ("turn", 1), ("weigh", 0), ("turn", 2), ("weigh", 1), ("turn", 3),
                   ("V", 0, 10), ("V", 1, 11), ("weigh", 2), ("Y", 0, 12), ("weigh", 3),
                   ("V", 2, 13), ("V", 3, 14), ("Y", 1, 15)])

        def plan(last):
            if not last:
                return PLAN
            work = [w for w in PLAN if w[0] in ("score", "turn", "weigh")]
            at = work.index(("weigh", 3))
            return work[:at] + [("Y", 0, 0)] + work[at:] + [("Y", 1, 1)]

        def steps(eng, body):
            body(0, False)
            with eng.Fori(1, QUADS - 1) as i:
                body(i, False)
            body(QUADS - 1, True)

        block = ctx.enter_context(nc.Block())

        @block.sync
        def _(sp):
            for m, w in enumerate((awq, awk, awv)):
                sp.dma_start(raw[m][:, :, :], w.rearrange("(k p) n -> p k n", p=P)).then_inc(raw_in[m], 16)
            sp.dma_start(raw[3][:, :, :].rearrange("p a (b d) -> p (a b) d", d=D),
                         awo.rearrange("(k p) n -> p k n", p=P)).then_inc(raw_in[3], 16)

        @block.gpsimd
        def _(pool):
            def rstd_of(n):
                pool.wait_ge(ln_mv, 2 * n + 2)
                apart(pool, waited)
                pool.tensor_scalar(vare[:, :], mv[:, :, 1], LN_EPS, None, ALU.add).then_inc(ln_ve, 1)
                pool.wait_ge(ln_ve, n + 1)
                pool.tensor_tensor(rstd[:, :], vare[:, :], half[:, :], ALU.pow).then_inc(ln_rs, 1)

            def divide(i, s):
                pool.wait_ge(inverted, 4 * i + s + 1)
                rows = Pr[s][:, :, :, :].rearrange("p j b k -> p (j b) k")
                pool.tensor_tensor(rows, rows, rinv[s][:, :].unsqueeze(2).to_broadcast([P, 8, SQ]), ALU.mult
                                   ).then_inc(weighted, 1)

            rstd_of(0)

            def body(i, last):
                if not last:
                    rstd_of(i + 1)
                for s in range(4):
                    divide(i, s)

            steps(pool, body)

        @block.tensor
        def _(pe):
            def parts(m, cols=slice(None)):
                return [(m[HI][:, k, cols], m[LO][:, k, cols]) for k in range(m[HI].shape[1])]

            def bank_read(kind, part, quad):
                if kind == "X":
                    pe.wait_ge(xt_lo, 2 * quad + part + 1)
                elif kind == "Y":
                    pe.wait_ge(x_done, 2 * quad + part + 1)
                else:
                    pe.wait_ge(by_dve if part % 2 else by_act, COPIES * quad + "QKV".index(kind) * 2 + part // 2 + 1)

            def fill(bank, kind, part, quad):
                out = pJ[bank]
                if kind == "X":
                    pe.wait_ge(ln_xn, 2 * quad + 2)
                    for t in range(2):
                        last = pe.transpose(out[:, P * t:P * t + P], XN[:, t, P * part:P * part + P], ident[:, :])
                elif kind in "QK":
                    w = W["QK".index(kind)]
                    pe.wait_ge(xt_lo, 2 * quad + 2)
                    for t in range(2):
                        j = 2 * part + t
                        last = split_matmul(pe, out[:, 256 * t:256 * t + 256], parts(w, slice(P * j, P * j + P)),
                                            parts(XT))
                elif kind == "V":
                    t, h = part // 2, part % 2
                    last = split_matmul(pe, out[:, :], parts(XT, slice(P * t, P * t + P)),
                                        parts(W[2], slice(512 * h, 512 * h + 512)))
                else:
                    pe.wait_ge(o_lo, 2 * (4 * quad + 2 * part + 2))
                    last = split_matmul(pe, out[:, 0:D], parts(OT[part]), parts(WO))
                last.then_inc(proj, 1)

            def score(i, s):
                t, h = s // 2, s % 2
                if s == 0:
                    pe.wait_ge(by_act, COPIES * i + 4)
                    pe.wait_ge(by_dve, COPIES * i + 4)
                after(pe, o_lo, 2 * (4 * i + s - 3))
                out = pS[s][:, :].rearrange("p (j b k) -> p j b k", j=4, b=2)
                pe.matmul(pS[s][:, :], identb[:, :], causal[:, :, :], start=True, stop=False, skip_group_check=True)
                for jq in range(4):
                    for b in range(2):
                        tok = slice(P * t + SQ * b, P * t + SQ * b + SQ)
                        for h2 in range(2):
                            rows = slice(E * h2, E * h2 + E)
                            last = pe.matmul(out[rows, jq, b, :], QT[rows, 4 * h + jq, tok], KT[rows, 4 * h + jq, tok],
                                             start=False, stop=True, skip_group_check=True)
                last.then_inc(scored, 1)

            def turn(i, s):
                pe.wait_ge(weighted, 4 * i + s + 1)
                for jq in range(4):
                    last = pe.transpose(pS[s][:, P * jq:P * jq + P], Pr[s][:, jq, :, :].rearrange("p b k -> p (b k)"),
                                        ident[:, :])
                last.then_inc(turned, 1)

            def weigh(i, s):
                t, h = s // 2, s % 2
                pe.wait_ge(pt_done, 4 * i + s + 1)
                if s == 0:
                    pe.wait_ge(by_act, COPIES * (i + 1))
                    pe.wait_ge(by_dve, COPIES * (i + 1))
                after(pe, o_lo, 2 * (4 * i + s - 1))
                apart(pe, waited)
                for jq in range(4):
                    for b in range(2):
                        keys = slice(SQ * b, SQ * b + SQ)
                        for h2 in range(2):
                            head = 2 * (4 * h + jq) + h2
                            last = pe.matmul(o_half(s, b)[E * h2:E * h2 + E, :, :][:, jq, :],
                                             V[keys, t, E * head:E * head + E],
                                             PT[s % 2][keys, jq, SQ * h2:SQ * h2 + SQ], start=True, stop=True)
                last.then_inc(pv_done, 1)

            pe.wait_ge(w_lo, 4)
            for k, (kind, part) in enumerate(AHEAD):
                if k >= 2:
                    bank_read(*AHEAD[k - 2], 0)
                fill(k % 2, kind, part, 0)

            def body(i, last):
                before = {}
                for work in plan(last):
                    kind, s = work[0], work[1]
                    if kind == "score":
                        score(i, s)
                    elif kind == "turn":
                        turn(i, s)
                    elif kind == "weigh":
                        weigh(i, s)
                    else:
                        k = work[2]
                        quad = i if kind == "Y" else i + 1
                        before[k] = (kind, s, quad)
                        if k < 2:
                            bank_read("V", 2, i)
                            bank_read("V", 3, i)
                            after(pe, x_done, 2 * i)
                        else:
                            bank_read(*before[k - 2])
                        fill(k % 2, kind, s, quad)

            steps(pe, body)

        def target(kind, part):
            if kind == "Q":
                return QT[:, 2 * part:2 * part + 2, :].rearrange("p j n -> p (j n)")
            if kind == "K":
                return KT[:, 2 * part:2 * part + 2, :].rearrange("p j n -> p (j n)")
            return V[:, part // 2, 512 * (part % 2):512 * (part % 2) + 512]

        def reused(eng, i, kind, part):
            if i is None:
                return
            if kind in "QK":
                eng.wait_ge(scored, 4 * i + 4)
            elif kind == "V":
                eng.wait_ge(pv_done, 4 * i + 2 * (part // 2) + 2)

        @block.scalar
        def _(act):
            def split_w(m):
                act.wait_ge(raw_in[m], 16)
                dst = WO[HI][:, :, :].rearrange("p j d -> p (j d)") if m == 3 else W[m][HI][:, :, :].rearrange(
                    "p k n -> p (k n)")
                act.activation(dst, raw[m][:, :, :].rearrange("p k n -> p (k n)"), ACT.Copy).then_inc(w_hi, 1)

            def x_high(r, part, bank):
                act.wait_ge(proj, r + 1)
                act.activation(XT[HI][:, part, :], pJ[bank][:, 0:2 * P], ACT.Copy).then_inc(xt_hi, 1)

            def copy(r, kind, part, bank, i):
                act.wait_ge(proj, r + 1)
                reused(act, i, kind, part)
                act.activation(target(kind, part), pJ[bank][:, :], ACT.Copy).then_inc(by_act, 1)

            def exps(i, s):
                act.wait_ge(shifted, 4 * i + s + 1)
                rows = Pr[s][:, :, :, :].rearrange("p j b k -> p (j b k)")
                act.activation(rows, rows, ACT.Exp, scale=E ** -0.5).then_inc(exped, 1)

            def copy_turned(i, s):
                act.wait_ge(turned, 4 * i + s + 1)
                after(act, pv_done, 4 * i + s - 1)
                act.activation(PT[s % 2][:, :, :].rearrange("p j n -> p (j n)"), pS[s][:, :], ACT.Copy
                               ).then_inc(pt_done, 1)

            def o_high(i, s):
                act.wait_ge(pv_done, 4 * i + s + 1)
                for b in range(2):
                    act.activation(OT[s // 2][HI][:, 4 * (s % 2):4 * (s % 2) + 4, SQ * b:SQ * b + SQ], o_half(s, b),
                                   ACT.Copy).then_inc(o_hi, 1)

            for m in range(4):
                split_w(m)
            for r, (kind, part) in enumerate(AHEAD):
                if kind == "X":
                    x_high(r, part, r % 2)
                elif part % 2 == 0:
                    copy(r, kind, part, r % 2, None)

            def body(i, last):
                r = EV0 + EV * i
                exps(i, 0)
                exps(i, 1)
                exps(i, 2)
                if not last:
                    x_high(r, 0, 0)
                    x_high(r + 1, 1, 1)
                exps(i, 3)
                if not last:
                    copy(r + 2, "Q", 0, 0, i)
                    copy(r + 4, "Q", 2, 0, i)
                    copy(r + 6, "K", 0, 0, i)
                    copy(r + 8, "K", 2, 0, i)
                copy_turned(i, 0)
                copy_turned(i, 1)
                o_high(i, 0)
                copy_turned(i, 2)
                o_high(i, 1)
                copy_turned(i, 3)
                if not last:
                    copy(r + 10, "V", 0, 0, i)
                o_high(i, 2)
                o_high(i, 3)
                if not last:
                    copy(r + 13, "V", 2, 1, i)

            steps(act, body)

        @block.vector
        def _(dve):
            def split_w(m):
                dve.wait_ge(w_hi, m + 1)
                high, low = (WO[HI], WO[LO]) if m == 3 else W[m]
                flat = "p j d -> p (j d)"
                dve.tensor_tensor(low[:, :, :].rearrange(flat), raw[m][:, :, :].rearrange(flat),
                                  f32(high[:, :, :]).rearrange(flat), ALU.subtract).then_inc(w_lo, 1)

            def statistics(quad):
                for t in range(2):
                    dve.bn_stats(stats[:, t, :], X[:, bass.ds(2 * quad + t, 1), :].rearrange("p a d -> p (a d)")
                                 ).then_inc(ln_st, 1)
                for t in range(2):
                    dve.wait_ge(ln_st, 2 * quad + t + 1)
                    apart(dve, waited)
                    dve.bn_aggr(mv[:, t, :], stats[:, t, :]).then_inc(ln_mv, 1)

            def normalize(quad):
                dve.wait_ge(ln_rs, quad + 1)
                for t in range(2):
                    dve.tensor_scalar(XN[:, t, :], X[:, bass.ds(2 * quad + t, 1), :].rearrange("p a d -> p (a d)"),
                                      mv[:, t, 0:1], rstd[:, t:t + 1], ALU.subtract, ALU.mult).then_inc(ln_xn, 1)

            def x_low(quad, part, bank):
                dve.wait_ge(xt_hi, 2 * quad + part + 1)
                dve.tensor_tensor(XT[LO][:, part, :], pJ[bank][:, 0:2 * P], f32(XT[HI][:, part, :]), ALU.subtract
                                  ).then_inc(xt_lo, 1)

            def copy(r, kind, part, bank, i):
                dve.wait_ge(proj, r + 1)
                reused(dve, i, kind, part)
                dve.tensor_copy(target(kind, part), pJ[bank][:, :]).then_inc(by_dve, 1)

            def shift(i, s):
                n = 4 * i + s
                dve.wait_ge(scored, n + 1)
                after(dve, shifted, n)
                scores = pS[s][:, :].rearrange("p (j k) -> p j k", k=SQ)
                dve.tensor_reduce(rmax[:, :], scores, AX.X, ALU.max).then_inc(maxed, 1)
                dve.wait_ge(maxed, n + 1)
                dve.tensor_tensor(Pr[s][:, :, :, :].rearrange("p j b k -> p (j b) k"), scores,
                                  rmax[:, :].unsqueeze(2).to_broadcast([P, 8, SQ]), ALU.subtract).then_inc(shifted, 1)

            def sums(i, s):
                dve.wait_ge(exped, 4 * i + s + 1)
                dve.tensor_reduce(rsum[s][:, :], Pr[s][:, :, :, :].rearrange("p j b k -> p (j b) k"), AX.X, ALU.add
                                  ).then_inc(summed, 1)
                dve.wait_ge(summed, 4 * i + s + 1)
                dve.reciprocal(rinv[s][:, :], rsum[s][:, :]).then_inc(inverted, 1)

            def o_low(i, s):
                hs = slice(4 * (s % 2), 4 * (s % 2) + 4)
                for b in range(2):
                    dve.wait_ge(o_hi, 2 * (4 * i + s) + b + 1)
                    toks = slice(SQ * b, SQ * b + SQ)
                    dve.tensor_tensor(OT[s // 2][LO][:, hs, toks], o_half(s, b), f32(OT[s // 2][HI][:, hs, toks]),
                                      ALU.subtract).then_inc(o_lo, 1)

            def add_rows(r, i, t, bank):
                dve.wait_ge(proj, r + 1)
                rows = X[:, bass.ds(2 * i + t, 1), :].rearrange("p a d -> p (a d)")
                dve.tensor_tensor(rows, pJ[bank][:, 0:D], rows, ALU.add).then_inc(x_done, 1)

            statistics(0)
            normalize(0)
            for m in range(4):
                split_w(m)
            for r, (kind, part) in enumerate(AHEAD):
                if kind == "X":
                    x_low(0, part, r % 2)
                elif part % 2:
                    copy(r, kind, part, r % 2, None)

            def body(i, last):
                r = EV0 + EV * i
                if not last:
                    statistics(i + 1)
                shift(i, 0)
                if not last:
                    normalize(i + 1)
                shift(i, 1)
                sums(i, 0)
                shift(i, 2)
                sums(i, 1)
                shift(i, 3)
                if not last:
                    x_low(i + 1, 0, 0)
                    x_low(i + 1, 1, 1)
                sums(i, 2)
                sums(i, 3)
                if not last:
                    copy(r + 3, "Q", 1, 1, i)
                    copy(r + 5, "Q", 3, 1, i)
                    copy(r + 7, "K", 1, 1, i)
                    copy(r + 9, "K", 3, 1, i)
                o_low(i, 0)
                o_low(i, 1)
                if not last:
                    copy(r + 11, "V", 1, 1, i)
                o_low(i, 2)
                if last:
                    add_rows(r, i, 0, 0)
                else:
                    add_rows(r + 12, i, 0, 0)
                o_low(i, 3)
                if last:
                    add_rows(r + 1, i, 1, 1)
                else:
                    copy(r + 14, "V", 3, 0, i)
                    add_rows(r + 15, i, 1, 1)

            steps(dve, body)


def feed_forward(nc, X, ident, identb, w_inT, b_in, w_out, b_out, out):
    G = 512
    GROUPS = TOK // G
    GT = G // P
    FK = FF // P
    with ExitStack() as ctx:
        def sb(name, shape, dt):
            return ctx.enter_context(nc.sbuf_tensor("f_" + name, shape, dt))

        def sem(name):
            return ctx.enter_context(nc.semaphore("f_" + name))

        raw = [sb(f"raw_{n}", [P, FK, D], F32) for n in ("in", "out")]
        bias_in = sb("bias_in", [P, FK], F32)
        bias_out = sb("bias_out", [P, D], F32)
        w_max = sb("w_max", [P, 2, FK], F32)
        w_scale = sb("w_scale", [P, 2, FK], F32)
        w_step = sb("w_step", [P, 2, FK], F32)
        quotient = [sb(f"quotient_{n}", [P, 2 * FK], F32) for n in ("r", "a_lo", "q_lo", "left", "part")]
        quotient_high = [sb(f"quotient_{n}", [P, 2 * FK], F32R) for n in ("a_hi", "q_hi")]
        WIq = sb("WIq", [P, FK, D], BF16)
        WI = sb("WI", [P, KC, FF], BF16)
        WO = sb("WO", [P, FK, D], F32R)
        minus_half = sb("minus_half", [P, TILES], F32)
        stats = sb("stats", [P, TILES, 6], F32)
        mv = sb("mv", [P, TILES, 2], F32)
        vare = sb("vare", [P, TILES], F32)
        rstd = sb("rstd", [P, TILES], F32)
        XN = sb("XN", [P, TILES, D], F32)
        XQ = sb("XQ", [P, GT, D], F32)
        x_tile_max = sb("x_tile_max", [P, GROUPS], F32)
        h_tile_max = sb("h_tile_max", [P, FK * GROUPS], F32)
        part_max = [sb(f"part_max_{n}", [P, 1], F32) for n in "xh"]
        all_max = [sb(f"all_max_{n}", [P, 1], F32) for n in "xh"]
        a_max = [sb(f"a_max_{n}", [P, 1], F32) for n in "xh"]
        a_scale = [sb(f"a_scale_{n}", [P, 1], F32) for n in "xh"]
        a_step = [sb(f"a_step_{n}", [P, 1], F32) for n in "xh"]
        h_step = sb("h_step", [P, FK], F32)
        round_up = sb("round_up", [P, 1], F32)
        XT = [sb(f"XT{s}", [P, KC, TOK], BF16) for s in "hl"]
        Hid = sb("Hid", [P, FK, TOK], F32)
        RING = 4
        GT_ = [[sb(f"G{r}{s}", [P, G], F32R) for s in "hl"] for r in range(RING)]

        bank = [ctx.enter_context(nc.psum_tensor(f"f_bank{n}", [P, G], F32)) for n in range(7)]
        bankb = ctx.enter_context(nc.psum_tensor("f_bankb", [P, 2 * G], BF16))
        HB = 4

        w_in, w_out_in, bi_in, bo_in = sem("w_in"), sem("w_out_in"), sem("bi_in"), sem("bo_in")
        made, made_w, q_w = sem("made"), sem("made_w"), sem("q_w")
        w_rounded = sem("w_rounded")
        w_turned, w_copied = sem("w_turned"), sem("w_copied")
        waited = sem("waited")
        ln_st, ln_mv, ln_ve, ln_rs, ln_xn = sem("ln_st"), sem("ln_mv"), sem("ln_ve"), sem("ln_rs"), sem("ln_xn")
        x_max, g_max, scaled, biased = sem("x_max"), sem("g_max"), sem("scaled"), sem("biased")
        rounded, x_turned, x_hi, x_lo = sem("rounded"), sem("x_turned"), sem("x_hi"), sem("x_lo")
        first, gelu_done, h_max = sem("first"), sem("gelu"), sem("h_max")
        h_rounded, h_scaled, g_hi, g_lo = sem("h_rounded"), sem("h_scaled"), sem("g_hi"), sem("g_lo")
        second, y_done, stored = sem("second"), sem("y"), sem("stored")
        CONST = 2

        block = ctx.enter_context(nc.Block())

        def steps(eng, body):
            body(0, False)
            with eng.Fori(1, GROUPS - 1) as g:
                body(g, False)
            body(GROUPS - 1, True)

        def tokens(g):
            return bass.ds(G * g, G)

        @block.sync
        def _(sp):
            rows = "(k p) d -> p k d"
            sp.dma_start(raw[0][:, :, :], w_inT.rearrange(rows, p=P)).then_inc(w_in, 16)
            sp.dma_start(raw[1][:, :, :], w_out.rearrange(rows, p=P)).then_inc(w_out_in, 16)
            sp.dma_start(bias_in[:, :], b_in).then_inc(bi_in, 16)
            sp.dma_start(bias_out[:, :], b_out.partition_broadcast(P)).then_inc(bo_in, 16)

            def body(g, last):
                sp.wait_ge(y_done, GT * g + GT)
                sp.dma_start(out.rearrange("(t p) d -> p t d", p=P)[:, bass.ds(GT * g, GT), :],
                             X[:, bass.ds(GT * g, GT), :]).then_inc(stored, 16)

            steps(sp, body)
            sp.wait_ge(stored, 16 * GROUPS)

        @block.gpsimd
        def _(pool):
            pool.memset(minus_half[:, :], -0.5).then_inc(made, 1)
            pool.memset(round_up[:, :], ROUND).then_inc(made, 1)
            pool.wait_ge(made, CONST)
            pool.wait_ge(ln_mv, TILES)
            pool.tensor_scalar(vare[:, :], mv[:, :, 1], LN_EPS, None, ALU.add).then_inc(ln_ve, 1)
            pool.wait_ge(ln_ve, 1)
            pool.tensor_tensor(rstd[:, :], vare[:, :], minus_half[:, :], ALU.pow).then_inc(ln_rs, 1)
            for n in range(2):
                pool.wait_ge(g_max, 2 * n + 1)
                pool.partition_all_reduce(all_max[n][:, :], part_max[n][:, :], P, RMAX).then_inc(g_max, 1)
                if n == 0:
                    pool.wait_ge(ln_xn, TILES)
                    pool.wait_ge(bo_in, 16)
                    for g in range(GROUPS):
                        tiles = X[:, GT * g:GT * g + GT, :]
                        pool.tensor_tensor(tiles, tiles, bias_out[:, :].unsqueeze(1).to_broadcast([P, GT, D]),
                                           ALU.add).then_inc(biased, 1)

        @block.tensor
        def _(pe):
            pe.wait_ge(q_w, 1)
            for k in range(KC):
                for f in range(FK):
                    last = pe.transpose(bankb[:, P * f:P * f + P], WIq[:, f, P * k:P * k + P], identb[:, :])
                last.then_inc(w_turned, 1)
                pe.wait_ge(w_copied, k + 1)

            def turn(g):
                pe.wait_ge(rounded, g + 1)
                after(pe, x_lo, 2 * g)
                for k in range(KC):
                    for t in range(GT):
                        last = pe.transpose(bank[HB + k][:, P * t:P * t + P], XQ[:, t, P * k:P * k + P], ident[:, :])
                    last.then_inc(x_turned, 1)

            turn(0)

            def hidden(g, last):
                pe.wait_ge(x_lo, 2 * g + 2)
                for f in range(FK):
                    n = FK * g + f
                    after(pe, gelu_done, n - HB + 1)
                    for k in range(KC):
                        for s in (HI, LO):
                            m = pe.matmul(bank[f % HB][:, :], WI[:, k, P * f:P * f + P], XT[s][:, k, tokens(g)],
                                          start=(k == 0 and s == HI), stop=(k == KC - 1 and s == LO))
                    m.then_inc(first, 1)
                    if f == 1 and not last:
                        turn(g + 1)

            steps(pe, hidden)

            pe.wait_ge(gelu_done, FK * GROUPS)

            def output(g, last):
                for f in range(FK):
                    pe.wait_ge(g_lo, FK * g + f + 1)
                    for t in range(GT):
                        if f == 0:
                            after(pe, y_done, GT * (g - 1) + t + 1)
                        for s in (HI, LO):
                            m = pe.matmul(bank[t][:, 0:D], GT_[f % RING][s][:, P * t:P * t + P], WO[:, f, :],
                                          start=(f == 0 and s == HI), stop=(f == FK - 1 and s == LO))
                    m.then_inc(second, 1)

            steps(pe, output)

        @block.scalar
        def _(act):
            for k in range(KC):
                act.wait_ge(w_turned, k + 1)
                act.activation(WI[:, k, :], bankb[:, :], ACT.Copy).then_inc(w_copied, 1)

            def x_high(g):
                for k in range(KC):
                    act.wait_ge(x_turned, KC * g + k + 1)
                    act.activation(XT[HI][:, k, tokens(g)], bank[HB + k][:, :], ACT.Copy, bias=-ROUND
                                   ).then_inc(x_hi, 1)

            x_high(0)
            act.wait_ge(bi_in, 16)
            act.wait_ge(scaled, 1)

            def hidden(g, last):
                for f in range(FK):
                    act.wait_ge(first, FK * g + f + 1)
                    act.activation(Hid[:, f, tokens(g)], bank[f % HB][:, :], ACT.Gelu, bias=bias_in[:, f:f + 1],
                                   scale=h_step[:, f:f + 1]).then_inc(gelu_done, 1)
                    if f == 2 and not last:
                        x_high(g + 1)

            steps(act, hidden)

            act.wait_ge(gelu_done, FK * GROUPS)
            act.wait_ge(scaled, 2)

            def output(g, last):
                def rounding(g, f):
                    act.activation(Hid[:, f, tokens(g)], Hid[:, f, tokens(g)], ACT.Identity, bias=round_up[:, 0:1],
                                   scale=a_scale[1][:, 0:1]).then_inc(h_rounded, 1)

                if isinstance(g, int) and g == 0:
                    rounding(0, 0)
                for f in range(FK):
                    if f < FK - 1:
                        rounding(g, f + 1)
                    elif not last:
                        rounding(g + 1, 0)
                    n = FK * g + f
                    act.wait_ge(h_scaled, n + 1)
                    after(act, second, n - RING + 1)
                    apart(act, waited)
                    act.activation(GT_[f % RING][HI][:, :], Hid[:, f, tokens(g)], ACT.Copy).then_inc(g_hi, 1)

            steps(act, output)

        @block.vector
        def _(dve):
            done = 0

            def in_turn(instruction):
                nonlocal done
                done += 1
                instruction.then_inc(made_w, 1)
                dve.wait_ge(made_w, done)

            def exact_quotient(q, numerator, a):
                r, a_lo, q_lo, left, part = (t[:, :] for t in quotient)
                a_hi, q_hi = (t[:, :] for t in quotient_high)
                in_turn(dve.reciprocal(r, a))
                in_turn(dve.tensor_scalar(q, r, numerator, None, ALU.mult))
                for value, high, low in ((a, a_hi, a_lo), (q, q_hi, q_lo)):
                    in_turn(dve.tensor_copy(high, value))
                    in_turn(dve.tensor_tensor(low, value, f32(high), ALU.subtract))
                in_turn(dve.tensor_tensor(part, f32(q_hi), f32(a_hi), ALU.mult))
                in_turn(dve.tensor_scalar(left, part, -1.0, numerator, ALU.mult, ALU.add))
                for one, other in ((f32(q_hi), a_lo), (q_lo, f32(a_hi)), (q_lo, a_lo)):
                    in_turn(dve.tensor_tensor(part, one, other, ALU.mult))
                    in_turn(dve.tensor_tensor(left, left, part, ALU.subtract))
                in_turn(dve.tensor_tensor(left, left, r, ALU.mult))
                in_turn(dve.tensor_tensor(q, q, left, ALU.add))

            for n, loaded in enumerate((w_in, w_out_in)):
                dve.wait_ge(loaded, 16)
                in_turn(dve.tensor_reduce(w_max[:, n, :], raw[n][:, :, :], AX.X, ALU.max, apply_absolute_value=True))
            flat = "p n f -> p (n f)"
            in_turn(dve.tensor_scalar(w_max[:, :, :], w_max[:, :, :], 1e-8, None, ALU.max))
            exact_quotient(w_scale[:, :, :].rearrange(flat), 127.0, w_max[:, :, :].rearrange(flat))
            in_turn(dve.reciprocal(w_step[:, :, :], w_scale[:, :, :]))
            for n, ints in enumerate((WIq, WO)):
                for f in range(FK):
                    m = dve.tensor_scalar(raw[n][:, f, :], raw[n][:, f, :], w_scale[:, n, f:f + 1], ROUND,
                                          ALU.mult, ALU.add)
                    m.then_inc(w_rounded, 1)
                dve.wait_ge(w_rounded, FK * (n + 1))
                dve.tensor_scalar(ints[:, :, :], raw[n][:, :, :], -ROUND, None, ALU.add).then_inc(q_w, 1)

            def tile(T, t):
                return T[:, bass.ds(t, 1), :].rearrange("p a d -> p (a d)")

            for t in range(TILES):
                dve.bn_stats(stats[:, t, :], X[:, t, :]).then_inc(ln_st, 1)
            for t in range(TILES):
                dve.wait_ge(ln_st, t + 1)
                dve.bn_aggr(mv[:, t, :], stats[:, t, :]).then_inc(ln_mv, 1)

            def normalize(g, last):
                for t in range(GT):
                    n = GT * g + t
                    dve.tensor_scalar(tile(XN, n), tile(X, n), mv[:, bass.ds(n, 1), 0:1].rearrange("p a d -> p (a d)"),
                                      rstd[:, bass.ds(n, 1)], ALU.subtract, ALU.mult).then_inc(ln_xn, 1)
                dve.wait_ge(ln_xn, GT * g + GT)
                dve.tensor_reduce(x_tile_max[:, bass.ds(g, 1)], XN[:, bass.ds(GT * g, GT), :], AX.XY, ALU.max,
                                  apply_absolute_value=True).then_inc(x_max, 1)

            def scale_of(n, maxima):
                dve.tensor_reduce(part_max[n][:, :], maxima[:, :], AX.X, ALU.max).then_inc(g_max, 1)
                dve.wait_ge(g_max, 2 * n + 2)
                in_turn(dve.tensor_scalar(a_max[n][:, :], all_max[n][:, :], 1e-8, None, ALU.max))
                in_turn(dve.reciprocal(a_step[n][:, :], a_max[n][:, :]))
                in_turn(dve.tensor_scalar(a_scale[n][:, :], a_step[n][:, :], 32767.0, None, ALU.mult))
                in_turn(dve.reciprocal(a_step[n][:, :], a_scale[n][:, :]))

            dve.wait_ge(made, CONST)
            dve.wait_ge(ln_mv, TILES)
            dve.wait_ge(ln_rs, 1)
            steps(dve, normalize)
            dve.wait_ge(x_max, GROUPS)
            scale_of(0, x_tile_max)
            dve.tensor_scalar(h_step[:, :], w_step[:, 0, :], a_step[0][:, 0:1], None, ALU.mult).then_inc(scaled, 1)

            def rounding(g):
                after(dve, x_turned, KC * g)
                dve.tensor_scalar(XQ[:, :, :], XN[:, bass.ds(GT * g, GT), :], a_scale[0][:, 0:1], ROUND, ALU.mult, ALU.add).then_inc(rounded, 1)

            def x_low(g):
                for k in range(KC):
                    dve.wait_ge(x_hi, KC * g + k + 1)
                    dve.scalar_tensor_tensor(XT[LO][:, k, tokens(g)], bank[HB + k][:, :], -ROUND,
                                             XT[HI][:, k, tokens(g)], ALU.add, ALU.subtract).then_inc(x_lo, 1)

            rounding(0)
            x_low(0)

            def hidden(g, last):
                if not last:
                    rounding(g + 1)
                for f in range(FK):
                    n = FK * g + f
                    dve.wait_ge(gelu_done, n + 1)
                    dve.tensor_reduce(h_tile_max[:, bass.ds(n, 1)], Hid[:, f, tokens(g)], AX.X, ALU.max,
                                      apply_absolute_value=True).then_inc(h_max, 1)
                    if f == 2 and not last:
                        x_low(g + 1)

            steps(dve, hidden)
            dve.wait_ge(h_max, FK * GROUPS)
            scale_of(1, h_tile_max)
            dve.sem_inc(scaled, 1)
            dve.wait_ge(biased, GROUPS)

            def output(g, last):
                def weighting(g, f):
                    dve.wait_ge(h_rounded, FK * g + f + 1)
                    dve.tensor_scalar(Hid[:, f, tokens(g)], Hid[:, f, tokens(g)], -ROUND, w_step[:, 1, f:f + 1],
                                      ALU.add, ALU.mult).then_inc(h_scaled, 1)

                if isinstance(g, int) and g == 0:
                    weighting(0, 0)
                for f in range(FK):
                    if f < FK - 1:
                        weighting(g, f + 1)
                    elif not last:
                        weighting(g + 1, 0)
                    dve.wait_ge(g_hi, FK * g + f + 1)
                    dve.tensor_tensor(GT_[f % RING][LO][:, :], Hid[:, f, tokens(g)], f32(GT_[f % RING][HI][:, :]),
                                      ALU.subtract).then_inc(g_lo, 1)
                dve.wait_ge(second, FK * g + FK)
                for t in range(GT):
                    rows = tile(X, GT * g + t)
                    dve.scalar_tensor_tensor(rows, bank[t][:, 0:D], a_step[1][:, 0:1], rows, ALU.mult, ALU.add
                                             ).then_inc(y_done, 1)

            steps(dve, output)


def kernel(x, ctx_1024, mask_B_ik0, L0_xattn_Wq, L0_xattn_Wk, L0_xattn_Wv, L0_xattn_Wo, L0_attn_wq, L0_attn_wk,
           L0_attn_wv, L0_attn_wo, L0_ffn_W_in, L0_ffn_b_in, L0_ffn_W_out, L0_ffn_b_out):
    import numpy as np
    import concourse.bacc as bacc
    from concourse.bass_utils import run_bass_kernel_spmd

    def by_model_width(w):
        return np.asarray(w).reshape(HE, D).T

    laid_out = {
        "x": np.asarray(x).reshape(TOK, D),
        "ctxT": np.asarray(ctx_1024).transpose(2, 0, 1).reshape(D, B * SK),
        "xwq": L0_xattn_Wq, "xwk": L0_xattn_Wk, "xwv": L0_xattn_Wv, "xwo": L0_xattn_Wo,
        "awq": by_model_width(L0_attn_wq), "awk": by_model_width(L0_attn_wk), "awv": by_model_width(L0_attn_wv),
        "awo": np.asarray(L0_attn_wo).T,
        "w_inT": np.asarray(L0_ffn_W_in).T,
        "b_in": np.asarray(L0_ffn_b_in).reshape(FF // P, P).T,
        "w_out": L0_ffn_W_out,
        "b_out": L0_ffn_b_out,
    }
    nc = bacc.Bacc("TRN2", target_bir_lowering=False, num_devices=1)
    arrays, args = {}, {}
    for name, a in laid_out.items():
        arrays[name] = np.ascontiguousarray(a)
        args[name] = nc.dram_tensor(name, arrays[name].shape, F32, kind="ExternalInput").ap()
    out = nc.dram_tensor("out", (TOK, D), F32, kind="ExternalOutput").ap()
    build(nc, **args, out=out)
    result = run_bass_kernel_spmd(nc, [arrays], core_ids=[0])
    return result.results[0]["out"].reshape(B, SQ, D)
```

```python
from contextlib import ExitStack

import concourse.bass as bass
from concourse import mybir

ALU = mybir.AluOpType
ACT = mybir.ActivationFunctionType
AX = mybir.AxisListType
F32 = mybir.dt.float32
F32R = mybir.dt.float32r
BF16 = mybir.dt.bfloat16
RMAX = bass.bass_isa.ReduceOp.max

P = 128
B, SQ, D, SK = 32, 64, 256, 256
H = 16
XE = D // H
E = 64
HE = H * E
FF = 1024
TOK = B * SQ
TILES = TOK // P
QUADS = TILES // 2
KC = D // P
HP = H // 2
HI, LO = 0, 1
CONSTS = 7
LN_EPS = 1e-5
MASKED = -1e9 * 8.0
ROUND = 1.5 * 2.0 ** 23


def after(eng, sem, n):
    if isinstance(n, int) and n <= 0:
        return
    eng.wait_ge(sem, n)


def apart(eng, waited):
    eng.sem_inc(waited, 1)


def f32(ap):
    return ap.bitcast(F32)


def split_matmul(pe, out, w, x):
    n = len(w)
    for k in range(n):
        (wh, wl), (xh, xl) = w[k], x[k]
        pe.matmul(out, wh, xh, start=(k == 0), stop=False)
        pe.matmul(out, wh, xl, start=False, stop=False)
        last = pe.matmul(out, wl, xh, start=False, stop=(k == n - 1))
    return last


def build(nc, x, ctxT, xwq, xwk, xwv, xwo, awq, awk, awv, awo, w_inT, b_in, w_out, b_out, out):
    with ExitStack() as whole:
        def keep(name, shape, dt):
            return whole.enter_context(nc.sbuf_tensor(name, shape, dt))

        X = keep("X", [P, TILES, D], F32)
        ident = keep("ident", [P, P], F32)
        identb = keep("identb", [P, P], BF16)
        causal = keep("causal", [P, HP, SQ], BF16)
        half = keep("half", [P, 2], F32)
        raw = keep("raw", [P, 4, KC * HE], F32)
        XN3 = raw[:, 2:4, :].rearrange("p a (t d) -> p (a t) d", d=D)
        ffn = Ffn(
            WI=keep("WIq", [P, FF // P, D], BF16),
            WO=keep("WO_ints", [P, FF // P, D], F32R),
            w_max=keep("w_max", [P, 2, FF // P], F32),
            w_scale=keep("w_scale", [P, 2, FF // P], F32),
            w_step=keep("w_step", [P, 2, FF // P], F32),
            x_tile_max=keep("x_tile_max", [P, QUADS], F32),
            XN=XN3)
        raw_in = [whole.enter_context(nc.semaphore(f"raw_in{m}")) for m in range(4)]
        cross_attention(nc, X, ident, identb, causal, half, x, ctxT, xwq, xwk, xwv, xwo,
                        raw, raw_in, (awq, awk, awv, awo))
        self_attention(nc, X, ident, identb, causal, half, raw, raw_in, ffn, w_inT, w_out)
        feed_forward(nc, X, ident, identb, half, ffn, b_in, b_out, out)


class Ffn:

    def __init__(self, **tensors):
        self.WI, self.WO = tensors["WI"], tensors["WO"]
        self.w_max, self.w_scale, self.w_step = tensors["w_max"], tensors["w_scale"], tensors["w_step"]
        self.XN, self.x_tile_max = tensors["XN"], tensors["x_tile_max"]


def statistics_of(dve, stats, mv, X, quad, stats_done, mv_done, waited):
    for t in range(2):
        dve.bn_stats(stats[:, t, :], X[:, bass.ds(2 * quad + t, 1), :].rearrange("p a d -> p (a d)")
                     ).then_inc(stats_done, 1)
    for t in range(2):
        dve.wait_ge(stats_done, 2 * quad + t + 1)
        apart(dve, waited)
        dve.bn_aggr(mv[:, t, :], stats[:, t, :]).then_inc(mv_done, 1)


def rstd_of_quad(pool, vare, rstd, mv, half, quad, mv_done, vare_done, rstd_done, waited):
    pool.wait_ge(mv_done, 2 * quad + 2)
    apart(pool, waited)
    pool.tensor_scalar(vare[:, :], mv[:, :, 1], LN_EPS, None, ALU.add).then_inc(vare_done, 1)
    pool.wait_ge(vare_done, quad + 1)
    pool.tensor_tensor(rstd[:, :], vare[:, :], half[:, :], ALU.pow).then_inc(rstd_done, 1)


def constants(pool, consts, ident, identb, causal, half):
    made = 0

    def in_turn(instruction):
        nonlocal made
        made += 1
        instruction.then_inc(consts, 1)
        pool.wait_ge(consts, made)

    in_turn(pool.memset(ident[:, :], 0.0))
    in_turn(pool.affine_select(out=ident[:, :], in_=ident[:, :], compare_op=ALU.not_equal, fill=1.0,
                               base=0, pattern=[[-1, P]], channel_multiplier=1))
    in_turn(pool.tensor_copy(identb[:, :], ident[:, :]))
    in_turn(pool.memset(half[:, :], -0.5))
    in_turn(pool.memset(causal[:, :, :], 0.0))
    for s in range(2):
        rows = slice(64 * s, 64 * s + 64)
        in_turn(pool.affine_select(out=causal[rows], in_=causal[rows], compare_op=ALU.is_ge, fill=MASKED,
                                   base=0, pattern=[[0, HP], [-1, SQ]], channel_multiplier=1))
    assert made == CONSTS


def cross_attention(nc, X, ident, identb, causal, half, x, ctxT, xwq, xwk, xwv, xwo,
                    raw, raw_in, later_weights):
    CK = SK
    PK = 2 * CK
    KT = CK // P
    CHUNKS = 8
    PAIRS = TILES
    EV = 10
    EV0 = 8
    RESTACK = 12 * 16
    W_ORDER = (1, 0, 2, 3)
    with ExitStack() as ctx:
        def sb(name, shape, dt):
            return ctx.enter_context(nc.sbuf_tensor(name, shape, dt))

        def ps(name, shape):
            return ctx.enter_context(nc.psum_tensor(name, shape, F32))

        def sem(name):
            return ctx.enter_context(nc.semaphore("x_" + name))

        wraw = sb("wraw", [P, 4, KC, D], F32)
        W = [sb(f"W{s}", [P, 4, KC, D], F32R) for s in "hl"]
        CT = [sb(f"CT{i}", [P, KC, PK], F32) for i in range(2)]
        CS = [sb(f"CS{s}", [P, KC, PK], F32R) for s in "hl"]
        stats = sb("stats", [P, 2, 6], F32)
        mv = sb("mv", [P, 2, 2], F32)
        vare = sb("vare", [P, 2], F32)
        rstd = sb("rstd", [P, 2], F32)
        XN = sb("XN", [P, 2, D], F32)
        XT = [sb(f"XT{s}", [P, KC, 2 * P], F32R) for s in "hl"]
        QS = [sb(f"QS{s}", [P, 2, 2, 2, SQ], F32R) for s in "hl"]
        KS = [sb(f"KS{s}", [P, 2, PK], F32R) for s in "hl"]
        Kst = [sb(f"Kst{i}", [96, HP, PK], F32R) for i in range(2)]
        Qraw = sb("Qraw", [96, 4, 2, 2, 2, SQ], F32)
        rows_of = sb("rows_of", [P, 2], F32)
        Qst = [sb(f"Qst{i}", [96, 4, 2, 2, 2, SQ], F32R) for i in range(2)]
        V = [sb(f"V{i}", [P, 2 * KT, D], F32) for i in range(2)]
        nmax = [sb(f"nmax{i}", [P, 2], F32) for i in range(2)]
        Pr = [sb(f"Pr{i}", [P, 2, CK], F32) for i in range(2)]
        rsum = [sb(f"rsum{i}", [P, 2], F32) for i in range(2)]
        rinv = [sb(f"rinv{i}", [P, 2], F32) for i in range(2)]
        PT = [sb(f"PT{i}", [P, 2, KT, P], F32) for i in range(2)]
        Oeven = sb("Oeven", [P, 2, 2, SQ], F32)
        Osum = sb("Osum", [P, 2, 2, SQ], F32)
        OT = [sb(f"OT{s}", [P, 2, P], F32R) for s in "hl"]

        pS = [ps(f"pS{i}", [P, 2, CK]) for i in range(2)]
        pT = [ps(f"pT{i}", [P, 2, KT, P]) for i in range(2)]
        pJ = [ps(f"pJ{i}", [P, 512]) for i in range(2)]
        pO = ps("pO", [P, 2, 2, 2, SQ])
        pY = ps("pY", [P, D])

        x_in0, x_in = sem("x_in0"), sem("x_in")
        w_in = [sem(f"w_in{m}") for m in range(4)]
        w_hi, w_lo = sem("w_hi"), sem("w_lo")
        ctx_in = [sem(f"ctx_in{i}") for i in range(2)]
        ctx_hi, ctx_lo = sem("ctx_hi"), sem("ctx_lo")
        consts = sem("consts")
        waited = sem("waited")
        ln_st, ln_mv, ln_ve, ln_rs, ln_xn = sem("ln_st"), sem("ln_mv"), sem("ln_ve"), sem("ln_rs"), sem("ln_xn")
        proj, hi, lo = sem("proj"), sem("hi"), sem("lo")
        kst_in = [sem(f"kst_in{i}") for i in range(2)]
        qraw_pool = sem("qraw_pool")
        qraw_in, q_taken, q_half, rows_made = sem("qraw_in"), sem("q_taken"), sem("q_half"), sem("rows_made")
        scores, maxed, exped, turned = sem("scores"), sem("maxed"), sem("exped"), sem("turned")
        scaled, pt_done, pv_done = sem("scaled"), sem("pt"), sem("pv")
        inverted, o_even, merged = sem("inverted"), sem("o_even"), sem("merged")
        oth, otl, y_done, x_done = sem("oth"), sem("otl"), sem("y"), sem("x")

        AHEAD = [("K", 0, 0), ("K", 0, 1), ("X", 0, 0), ("Q", 0, 0), ("V", 0, 0), ("V", 0, 1), ("K", 1, 0), ("K", 1, 1)]
        EVENTS = {0: (0, "V", 1, 0), 1: (1, "X", 2, 0), 2: (2, "V", 1, 1), 3: (3, "Q", 2, 0), 5: (4, "K", 2, 0),
                  6: (5, "K", 2, 1), 8: (6, "V", 2, 0), 9: (7, "V", 2, 1), 13: (8, "K", 3, 0), 14: (9, "K", 3, 1)}

        def event(i, c, last):
            if c not in EVENTS:
                return None
            k, kind, ahead, part = EVENTS[c]
            if last:
                if ahead > 1:
                    return None
                k = part
            return EV0 + EV * i + k, k, kind, ahead, part

        def steps(eng, body):
            body(0, False)
            with eng.Fori(1, QUADS - 1) as i:
                body(i, False)
            body(QUADS - 1, True)

        def q_restacked(eng, quads):
            eng.wait_ge(qraw_pool, RESTACK // 2)
            eng.wait_ge(qraw_in, RESTACK * quads - RESTACK // 2)

        def restack_q(eng, done, r, quads_taken, groups=range(4)):
            after(eng, lo, r + 1)
            apart(eng, waited)
            after(eng, q_taken, 2 * quads_taken)
            for jj in groups:
                for u, part in enumerate((HI, LO, HI)):
                    eng.dma_start(Qraw[32 * u:32 * u + 32, jj],
                                  f32(QS[part][32 * jj:32 * jj + 32])).then_inc(done, 16)

        block = ctx.enter_context(nc.Block())

        @block.sync
        def _(sp):
            def load_x(n):
                sp.dma_start(X[:, 4 * n:4 * n + 4, :],
                             x[4 * P * n:4 * P * (n + 1), :].rearrange("(t p) d -> p t d", p=P)
                             ).then_inc(x_in if n else x_in0, 16)

            def load_w(m):
                sp.dma_start(wraw[:, m], (xwq, xwk, xwv, xwo)[m].rearrange("(k p) n -> p k n", p=P)
                             ).then_inc(w_in[m], 16)

            load_w(W_ORDER[0])
            load_x(0)
            for m in W_ORDER[1:]:
                load_w(m)
            for n in range(1, 4):
                load_x(n)

            def restack_k(b, r, chunks_done):
                after(sp, lo, r + 1)
                apart(sp, waited)
                after(sp, scores, chunks_done)
                for jj in range(4):
                    for u, part in enumerate((HI, HI, LO)):
                        sp.dma_start(f32(Kst[b][32 * u:32 * u + 32, jj:HP:4, :]),
                                     f32(KS[part][32 * jj:32 * jj + 32, :, :])).then_inc(kst_in[b], 16)

            restack_k(0, 1, 0)
            restack_q(sp, qraw_in, 3, 0, (2, 3))
            restack_k(1, 7, 0)
            for m, w in enumerate(later_weights):
                sp.dma_start(raw[:, m, :].rearrange("p (k n) -> p k n", n=w.shape[1]),
                             w.rearrange("(k p) n -> p k n", p=P)).then_inc(raw_in[m], 16)

            def body(i, last):
                p = 2 * i
                if not last:
                    restack_q(sp, qraw_in, EV0 + EV * i + 3, i + 1)
                    restack_k(0, EV0 + EV * i + 5, CHUNKS * (p + 1))
                    restack_k(1, EV0 + EV * i + 9, CHUNKS * (p + 2))

            steps(sp, body)

        @block.gpsimd
        def _(pool):
            constants(pool, consts, ident, identb, causal, half)

            def rstd_of(n):
                rstd_of_quad(pool, vare, rstd, mv, half, n, ln_mv, ln_ve, ln_rs, waited)

            def ctx_low(b, n):
                pool.wait_ge(ctx_hi, n)
                pool.tensor_tensor(CS[LO][:, :, :], CT[b][:, :, :], f32(CS[HI][:, :, :]), ALU.subtract
                                   ).then_inc(ctx_lo, 1)

            def take_q(r, quad, chunks_done):
                q_restacked(pool, quad + 1)
                after(pool, scores, chunks_done)
                for h2 in range(2):
                    last = pool.tensor_tensor(
                        Qst[r][:, :, :, :, h2, :].rearrange("p j g a q -> p (j g a) q"),
                        Qraw[:, :, r].rearrange("p j g a q -> p j (g a) q"),
                        rows_of[0:96, h2:h2 + 1].unsqueeze(2).unsqueeze(3).to_broadcast([96, 4, 4, SQ]), ALU.mult)
                    if h2 == 0:
                        last.then_inc(q_half, 1)
                last.then_inc(q_taken, 1)

            rstd_of(0)
            for u in range(4):
                rows = rows_of[32 * u:32 * u + 32, :]
                pool.memset(rows, 1.0).then_inc(rows_made, 1)
                pool.wait_ge(rows_made, 3 * u + 1)
                pool.affine_select(out=rows, in_=rows, compare_op=ALU.is_ge, fill=0.0,
                                   base=0, pattern=[[-XE, 2]], channel_multiplier=1).then_inc(rows_made, 1)
                pool.wait_ge(rows_made, 3 * u + 2)
                pool.affine_select(out=rows, in_=rows, compare_op=ALU.is_ge, fill=0.0,
                                   base=XE - 1, pattern=[[XE, 2]], channel_multiplier=-1).then_inc(rows_made, 1)
                pool.wait_ge(rows_made, 3 * u + 3)
            restack_q(pool, qraw_pool, 3, 0, (0, 1))
            take_q(0, 0, 0)
            ctx_low(1, 2)
            take_q(1, 0, 0)

            def body(i, last):
                if not (isinstance(i, int) and i == 0):
                    take_q(1, i, CHUNKS * 2 * i)
                if not last:
                    rstd_of(i + 1)
                if not last:
                    ctx_low(0, 2 * i + 3)
                    take_q(0, i + 1, CHUNKS * (2 * i + 1))
                    ctx_low(1, 2 * i + 4)

            steps(pool, body)

        @block.tensor
        def _(pe):
            def parts(ts, cols=slice(None)):
                return [(ts[HI][:, k, cols], ts[LO][:, k, cols]) for k in range(KC)]

            def weights(m, cols=slice(None)):
                return [(W[HI][:, m, k, cols], W[LO][:, m, k, cols]) for k in range(KC)]

            def project(r, k_, kind, part, pair, q_needs=None):
                after(pe, lo, r - 1)
                bank = pJ[k_ % 2]
                if kind == "X":
                    pe.wait_ge(ln_xn, pair + 2)
                    for k in range(KC):
                        for t in range(2):
                            last = pe.transpose(bank[:, 256 * k + P * t:256 * k + P * t + P],
                                                XN[:, t, P * k:P * k + P], ident[:, :])
                elif kind == "Q":
                    pe.wait_ge(lo, q_needs)
                    for g in range(2):
                        last = split_matmul(pe, bank[:, 256 * g:256 * g + 256], weights(0, slice(P * g, P * g + P)),
                                            parts(XT))
                elif kind == "K":
                    pe.wait_ge(ctx_lo, pair + 1)
                    last = split_matmul(pe, bank[:, :], weights(1, slice(P * part, P * part + P)), parts(CS))
                else:
                    for t in range(2):
                        keys = slice(P * (2 * part + t), P * (2 * part + t) + P)
                        last = split_matmul(pe, bank[:, 256 * t:256 * t + 256], parts(CS, keys), weights(2))
                last.then_inc(proj, 1)

            def score(i, s):
                par, c = s // 8 % 2, s % 8
                b, jj = c // 4, c % 4
                if c == 0:
                    pe.wait_ge(kst_in[par], RESTACK * (i + 1 + s // 16))
                    pe.wait_ge(q_taken, 2 * i + s // 8 + 1)
                after(pe, exped, 2 * (16 * i + s) - 2)
                for t in range(2):
                    j = 2 * jj + t
                    last = pe.matmul(pS[c % 2][:, t, :], Qst[par][:, j % 4, j // 4, b, :, :],
                                     Kst[par][:, j, CK * b:CK * b + CK], start=True, stop=True)
                last.then_inc(scores, 1)

            def turn(i, s):
                pe.wait_ge(scaled, 2 * (16 * i + s) + 2)
                after(pe, pt_done, 16 * i + s - 1)
                for t in range(2):
                    for k in range(KT):
                        last = pe.transpose(pT[s % 2][:, t, k, :], Pr[s % 2][:, t, P * k:P * k + P], ident[:, :])
                last.then_inc(turned, 1)

            def weigh(i, s, last):
                par, c = s // 8 % 2, s % 8
                b, jj = c // 4, c % 4
                pe.wait_ge(pt_done, 16 * i + s + 1)
                if c == 0:
                    first = isinstance(i, int) and i == 0
                    pe.wait_ge(lo, EV0 + EV * i + (2 if last else 3) if par else 6 if first else EV0 + EV * i - 2)
                    after(pe, merged, 2 * i + par)
                for t in range(2):
                    j = 2 * jj + t
                    for k in range(KT):
                        last = pe.matmul(pO[32 * (j % 4):32 * (j % 4) + 32, j // 4, b, :, :],
                                         V[par][:, KT * b + k, 32 * j:32 * j + 32], PT[c % 2][:, t, k, :],
                                         start=(k == 0), stop=(k == KT - 1), skip_group_check=True)
                last.then_inc(pv_done, 1)

            def project_out(pair):
                pe.wait_ge(otl, pair + 1)
                after(pe, x_done, pair)
                split_matmul(pe, pY[:, :], parts(OT), weights(3)).then_inc(y_done, 1)

            pe.wait_ge(consts, CONSTS)
            for r, (kind, ahead, part) in enumerate(AHEAD):
                if kind != "X":
                    pe.wait_ge(w_lo, W_ORDER.index("QKV".index(kind)) + 1)
                if r == 6:
                    score(0, 0)
                    score(0, 1)
                project(r, r, kind, part, ahead, 3)

            pe.wait_ge(w_lo, 4)

            def body(i, last):
                first = isinstance(i, int) and i == 0
                for s in range(16):
                    if not (last and s >= 14):
                        score(i, s + 2)
                    turn(i, s)
                    if event(i, s, last):
                        r, k, kind, ahead, part = event(i, s, last)
                        project(r, k, kind, part, 2 * i + ahead, r - 1)
                    if not (first and s == 0):
                        weigh(i, s - 1, last)
                    if s == 11 or (s == 3 and not first):
                        project_out(2 * i + (s - 11) // 8)

            steps(pe, body)
            weigh(QUADS - 1, 15, True)
            project_out(PAIRS - 1)

        def target(s_, kind, part):
            if kind == "X":
                return XT[s_][:, :, :], "p (k n) -> p k n", dict(k=KC)
            if kind == "Q":
                return (QS[s_][:, :, :, :, :].rearrange("p r g a q -> p g r (a q)"), "p (g r n) -> p g r n",
                        dict(g=2, r=2))
            return KS[s_][:, part, :], "p n -> p n", {}

        def reused(eng, i, kind, ahead):
            if i is None:
                if kind == "K" and ahead == 1:
                    eng.wait_ge(kst_in[0], RESTACK)
                return
            if kind == "K":
                eng.wait_ge(kst_in[(ahead - 1) % 2], RESTACK * (i + (ahead + 1) // 2))
            elif kind == "Q":
                q_restacked(eng, i + 1)
            elif kind == "V":
                after(eng, pv_done, CHUNKS * (2 * i + ahead - 1))

        @block.scalar
        def _(act):
            def load_ctx(pair, b, before):
                after(act, ctx_lo, before)
                act.dma_start(CT[b][:, :, :],
                              ctxT.rearrange("(k p) n -> p k n", p=P)[:, :, bass.ds(pair * PK, PK)]
                              ).then_inc(ctx_in[b], 16)

            def high(r, k, kind, ahead, part, i):
                act.wait_ge(proj, r + 1)
                reused(act, i, kind, ahead)
                bank = pJ[k % 2]
                if kind == "V":
                    act.activation(V[ahead % 2][:, 2 * part, :], bank[:, 0:D], ACT.Copy).then_inc(hi, 1)
                else:
                    dst, how, kw = target(HI, kind, part)
                    act.activation(dst, bank[:, :].rearrange(how, **kw) if kw else bank[:, :], ACT.Copy).then_inc(hi, 1)

            def ctx_high(b, loads, proj_done):
                act.wait_ge(ctx_in[b], 16 * loads)
                after(act, proj, proj_done)
                act.activation(CS[HI][:, :, :], CT[b][:, :, :], ACT.Copy).then_inc(ctx_hi, 1)

            def exps(i, s):
                c = s % 8
                act.wait_ge(maxed, 16 * i + s + 1)
                after(act, turned, 16 * i + s - 1)
                for t in range(2):
                    act.activation(Pr[c % 2][:, t, :], pS[c % 2][:, t, :], ACT.Exp, bias=nmax[c % 2][:, t:t + 1],
                                   accum_out=rsum[c % 2][:, t:t + 1]).then_inc(exped, 1)

            def copy_turned(i, s):
                act.wait_ge(turned, 16 * i + s + 1)
                after(act, pv_done, 16 * i + s - 1)
                act.activation(PT[s % 2][:, :, :, :], pT[s % 2][:, :, :, :], ACT.Copy).then_inc(pt_done, 1)

            def take_even(pair):
                act.wait_ge(pv_done, CHUNKS * (pair + 1))
                act.activation(Oeven[:, :, :, :], pO[:, :, :, 0, :], ACT.Copy, scale=rows_of[:, 0:1]
                               ).then_inc(o_even, 1)

            def o_high(pair):
                act.wait_ge(merged, pair + 1)
                after(act, y_done, pair)
                act.activation(OT[HI][:, :, :], Osum[:, :, :, :].rearrange("p g a q -> p g (a q)"), ACT.Copy
                               ).then_inc(oth, 1)

            load_ctx(0, 0, 0)
            load_ctx(1, 1, 0)
            def split_w(m):
                act.wait_ge(w_in[m], 16)
                act.activation(W[HI][:, m], wraw[:, m], ACT.Copy).then_inc(w_hi, 1)

            split_w(W_ORDER[0])
            ctx_high(0, 1, 0)
            for m in W_ORDER[1:]:
                split_w(m)
            act.wait_ge(rows_made, 12)
            for r, (kind, ahead, part) in enumerate(AHEAD):
                if r == 6:
                    ctx_high(1, 1, 6)
                    exps(0, 0)
                high(r, r, kind, ahead, part, None)

            def body(i, last):
                first = isinstance(i, int) and i == 0
                for s in range(16):
                    if s == 0 and not last:
                        load_ctx(2 * i + 2, 0, 2 * i + 1)
                    if s == 2 and not last:
                        load_ctx(2 * i + 3, 1, 2 * i + 2)
                    if not (last and s == 15):
                        exps(i, s + 1)
                    if s == 9 or (s == 1 and not first):
                        take_even(2 * i + (s - 9) // 8)
                    copy_turned(i, s)
                    if event(i, s - 1, last):
                        r, k, kind, ahead, part = event(i, s - 1, last)
                        high(r, k, kind, ahead, part, i)
                    if s == 10 or (s == 2 and not first):
                        o_high(2 * i + (s - 10) // 8)
                    if s == 3 and not last:
                        ctx_high(0, i + 2, EV0 + EV * i + 3)
                    if s == 10 and not last:
                        ctx_high(1, i + 2, EV0 + EV * i + 8)

            steps(act, body)
            take_even(PAIRS - 1)
            o_high(PAIRS - 1)

        @block.vector
        def _(dve):
            def low(r, k, kind, ahead, part, i):
                dve.wait_ge(hi, r + 1)
                reused(dve, i, kind, ahead)
                bank = pJ[k % 2]
                if kind == "V":
                    dve.tensor_copy(V[ahead % 2][:, 2 * part + 1, :], bank[:, D:2 * D]).then_inc(lo, 1)
                else:
                    dst, how, kw = target(LO, kind, part)
                    high = f32(target(HI, kind, part)[0])
                    dve.tensor_tensor(dst, bank[:, :].rearrange(how, **kw) if kw else bank[:, :], high,
                                      ALU.subtract).then_inc(lo, 1)

            def statistics(quad):
                statistics_of(dve, stats, mv, X, quad, ln_st, ln_mv, waited)

            def normalize(quad):
                dve.wait_ge(ln_rs, quad + 1)
                for t in range(2):
                    dve.tensor_scalar(XN[:, t, :], X[:, bass.ds(2 * quad + t, 1), :].rearrange("p a d -> p (a d)"),
                                      mv[:, t, 0:1], rstd[:, t:t + 1], ALU.subtract, ALU.mult).then_inc(ln_xn, 1)

            def row_max(i, s):
                dve.wait_ge(scores, 16 * i + s + 1)
                dve.tensor_reduce(nmax[s % 2][:, :], pS[s % 2][:, :, :], AX.X, ALU.max, negate=True).then_inc(maxed, 1)

            def scale(i, s):
                n = 16 * i + s
                dve.wait_ge(exped, 2 * n + 2)
                dve.reciprocal(rinv[s % 2][:, :], rsum[s % 2][:, :]).then_inc(inverted, 1)
                dve.wait_ge(inverted, n + 1)
                for t in range(2):
                    dve.tensor_scalar(Pr[s % 2][:, t, :], Pr[s % 2][:, t, :], rinv[s % 2][:, t:t + 1], None, ALU.mult
                                      ).then_inc(scaled, 1)

            def merge(pair):
                dve.wait_ge(o_even, pair + 1)
                after(dve, otl, pair)
                dve.scalar_tensor_tensor(Osum[:, :, :, :], pO[:, :, :, 1, :], rows_of[:, 1:2], Oeven[:, :, :, :],
                                         ALU.mult, ALU.add).then_inc(merged, 1)

            def o_low(pair):
                dve.wait_ge(oth, pair + 1)
                dve.tensor_tensor(OT[LO][:, :, :], Osum[:, :, :, :].rearrange("p g a q -> p g (a q)"),
                                  f32(OT[HI][:, :, :]), ALU.subtract).then_inc(otl, 1)

            def add_rows(pair):
                dve.wait_ge(y_done, pair + 1)
                rows = X[:, bass.ds(pair, 1), :].rearrange("p a d -> p (a d)")
                dve.tensor_tensor(rows, pY[:, :], rows, ALU.add).then_inc(x_done, 1)

            def split_w(n):
                m = W_ORDER[n]
                dve.wait_ge(w_hi, n + 1)
                dve.tensor_tensor(W[LO][:, m], wraw[:, m], f32(W[HI][:, m]), ALU.subtract).then_inc(w_lo, 1)

            dve.wait_ge(x_in0, 16)
            statistics(0)
            split_w(0)
            dve.wait_ge(ctx_hi, 1)
            dve.tensor_tensor(CS[LO][:, :, :], CT[0][:, :, :], f32(CS[HI][:, :, :]), ALU.subtract).then_inc(ctx_lo, 1)
            normalize(0)
            for n in range(1, 4):
                split_w(n)
            for r, (kind, ahead, part) in enumerate(AHEAD):
                if r == 6:
                    row_max(0, 0)
                    row_max(0, 1)
                    scale(0, 0)
                low(r, r, kind, ahead, part, None)
            dve.wait_ge(x_in, 48)

            def body(i, last):
                first = isinstance(i, int) and i == 0
                for s in range(16):
                    if s == 0 and not last:
                        statistics(i + 1)
                    if not (last and s >= 14):
                        row_max(i, s + 2)
                    if s == 9 or (s == 1 and not first):
                        merge(2 * i + (s - 9) // 8)
                    if not (last and s == 15):
                        scale(i, s + 1)
                    if event(i, s - 1, last):
                        r, k, kind, ahead, part = event(i, s - 1, last)
                        low(r, k, kind, ahead, part, i)
                    if s == 0 and not last:
                        normalize(i + 1)
                    if s == 10 or (s == 2 and not first):
                        o_low(2 * i + (s - 10) // 8)
                    if s == 12 or (s == 4 and not first):
                        add_rows(2 * i + (s - 12) // 8)

            steps(dve, body)
            merge(PAIRS - 1)
            o_low(PAIRS - 1)
            add_rows(PAIRS - 1)


def self_attention(nc, X, ident, identb, causal, half, raw, raw_in, ffn, w_inT, w_out):
    EV = 16
    EV0 = 10
    COPIES = 6
    QKV = [("Q", 0), ("Q", 1), ("Q", 2), ("Q", 3), ("K", 0), ("K", 1), ("K", 2), ("K", 3)]
    AHEAD = [("X", 0), ("X", 1)] + QKV
    SPLITS = {2: 1, 4: 2, 6: 3}
    BLOCK = 4 * 2 * SQ
    FK = FF // P
    with ExitStack() as ctx:
        def sb(name, shape, dt):
            return ctx.enter_context(nc.sbuf_tensor("a_" + name, shape, dt))

        def ps(name, shape):
            return ctx.enter_context(nc.psum_tensor("a_" + name, shape, F32))

        def sem(name):
            return ctx.enter_context(nc.semaphore("a_" + name))

        W = [[sb(f"W{m}{s}", [P, KC, HE], F32R) for s in "hl"] for m in range(3)]
        WO = [sb(f"WO{s}", [P, HP, D], F32R) for s in "hl"]
        stats = sb("stats", [P, 2, 6], F32)
        mv = sb("mv", [P, 2, 2], F32)
        vare = sb("vare", [P, 2], F32)
        rstd = sb("rstd", [P, 2], F32)
        stats3 = sb("stats3", [P, 2, 6], F32)
        mv3 = sb("mv3", [P, 2, 2], F32)
        vare3 = sb("vare3", [P, 2], F32)
        rstd3 = sb("rstd3", [P, 2], F32)
        quotient = [sb(f"quotient_{n}", [P, 2 * FK], F32) for n in ("r", "a_lo", "q_lo", "left", "part")]
        quotient_high = [sb(f"quotient_{n}", [P, 2 * FK], F32R) for n in ("a_hi", "q_hi")]
        XN = sb("XN", [P, 2, D], F32)
        XT = [sb(f"XT{s}", [P, KC, 2 * P], F32R) for s in "hl"]
        QT = sb("QT", [P, HP, 2 * P], F32)
        KT = sb("KT", [P, HP, 2 * P], F32)
        V = sb("V", [P, 2, HE], F32)
        rmax = sb("rmax", [P, 8], F32)
        Pr = [sb(f"Pr{s}", [P, 4, 2, SQ], F32) for s in range(4)]
        rsum = [sb(f"rsum{s}", [P, 8], F32) for s in range(4)]
        rinv = [sb(f"rinv{s}", [P, 8], F32) for s in range(4)]
        PT = [sb(f"PT{s}", [P, 4, P], F32) for s in range(2)]
        OT = [[sb(f"OT{t}{s}", [P, HP, P], F32R) for s in "hl"] for t in range(2)]

        pS = [ps(f"pS{s}", [P, BLOCK]) for s in range(4)]
        pJ = [ps(f"pJ{s}", [P, 512]) for s in range(2)]
        pO = [ps(f"pO{s}", [P, 4, P]) for s in range(2)]

        ffn_in = [sem(f"ffn_in{n}") for n in range(2)]
        made_w, w_rounded = sem("made_w"), sem("w_rounded")
        l3_st, l3_mv, l3_ve, l3_rs, l3_xn = sem("l3_st"), sem("l3_mv"), sem("l3_ve"), sem("l3_rs"), sem("l3_xn")
        w_hi, w_lo = sem("w_hi"), sem("w_lo")
        waited = sem("waited")
        ln_st, ln_mv, ln_ve, ln_rs, ln_xn = sem("ln_st"), sem("ln_mv"), sem("ln_ve"), sem("ln_rs"), sem("ln_xn")
        proj, xt_hi, xt_lo = sem("proj"), sem("xt_hi"), sem("xt_lo")
        by_act, by_dve = sem("by_act"), sem("by_dve")
        scored, maxed, shifted, exped, summed, inverted, weighted = (
            sem("scored"), sem("maxed"), sem("shifted"), sem("exped"), sem("summed"), sem("inverted"), sem("weighted"))
        turned, pt_done, pv_done, o_hi, o_lo, x_done = (
            sem("turned"), sem("pt"), sem("pv"), sem("o_hi"), sem("o_lo"), sem("x"))

        def o_half(s, b):
            bank = pS[s][:, :].rearrange("p (j n) -> p j n", j=4) if b else pO[s % 2][:, :, :]
            return bank[:, :, SQ * b:SQ * b + SQ]

        PLAN = [("score", 0), ("V", 0), ("score", 1), ("V", 1), ("score", 2), ("V", 2), ("score", 3), ("V", 3),
                ("X", 0), ("X", 1), ("turn", 0), ("Q", 0), ("turn", 1), ("Q", 1), ("weigh", 0), ("Q", 2),
                ("turn", 2), ("Q", 3), ("weigh", 1), ("K", 0), ("turn", 3), ("K", 1), ("Y", 0), ("weigh", 2),
                ("K", 2), ("weigh", 3), ("K", 3), ("Y", 1)]

        def plan(last):
            k, work = 0, []
            for kind, s in PLAN:
                if kind in ("score", "turn", "weigh"):
                    work.append((kind, s, None))
                elif not (last and kind in ("X", "Q", "K")):
                    work.append((kind, s, k))
                    k += 1
            return work

        def place(kind, part, last):
            return next(k for what, s, k in plan(last) if (what, s) == (kind, part))

        def steps(eng, body):
            body(0, False)
            with eng.Fori(1, QUADS - 1) as i:
                body(i, False)
            body(QUADS - 1, True)

        block = ctx.enter_context(nc.Block())

        @block.sync
        def _(sp):
            for n, w in enumerate((w_inT, w_out)):
                sp.wait_ge(w_lo, n + 1)
                sp.dma_start(raw[:, n, :].rearrange("p (k d) -> p k d", d=D),
                             w.rearrange("(k p) d -> p k d", p=P)).then_inc(ffn_in[n], 16)

        @block.gpsimd
        def _(pool):
            def rstd_of(n):
                rstd_of_quad(pool, vare, rstd, mv, half, n, ln_mv, ln_ve, ln_rs, waited)

            def divide(i, s):
                pool.wait_ge(inverted, 4 * i + s + 1)
                rows = Pr[s][:, :, :, :].rearrange("p j b k -> p (j b) k")
                pool.tensor_tensor(rows, rows, rinv[s][:, :].unsqueeze(2).to_broadcast([P, 8, SQ]), ALU.mult
                                   ).then_inc(weighted, 1)

            rstd_of(0)

            def body(i, last):
                if not last:
                    rstd_of(i + 1)
                if not (isinstance(i, int) and i == 0):
                    rstd_of_quad(pool, vare3, rstd3, mv3, half, i - 1, l3_mv, l3_ve, l3_rs, waited)
                for s in range(4):
                    divide(i, s)

            steps(pool, body)

        @block.tensor
        def _(pe):
            def parts(m, cols=slice(None)):
                return [(m[HI][:, k, cols], m[LO][:, k, cols]) for k in range(m[HI].shape[1])]

            def bank_read(kind, part, quad):
                if kind == "X":
                    pe.wait_ge(xt_lo, 2 * quad + part + 1)
                elif kind == "Y":
                    pe.wait_ge(x_done, 2 * quad + part + 1)
                else:
                    pe.wait_ge(by_dve if part % 2 else by_act, COPIES * quad + "QKV".index(kind) * 2 + part // 2 + 1)

            def fill(bank, kind, part, quad):
                out = pJ[bank]
                if kind == "X":
                    pe.wait_ge(ln_xn, 2 * quad + 2)
                    for t in range(2):
                        last = pe.transpose(out[:, P * t:P * t + P], XN[:, t, P * part:P * part + P], ident[:, :])
                elif kind in "QK":
                    w = W["QK".index(kind)]
                    pe.wait_ge(xt_lo, 2 * quad + 2)
                    for t in range(2):
                        j = 2 * part + t
                        last = split_matmul(pe, out[:, 256 * t:256 * t + 256], parts(w, slice(P * j, P * j + P)),
                                            parts(XT))
                elif kind == "V":
                    t, h = part // 2, part % 2
                    last = split_matmul(pe, out[:, :], parts(XT, slice(P * t, P * t + P)),
                                        parts(W[2], slice(512 * h, 512 * h + 512)))
                else:
                    pe.wait_ge(o_lo, 2 * (4 * quad + 2 * part + 2))
                    last = split_matmul(pe, out[:, 0:D], parts(OT[part]), parts(WO))
                last.then_inc(proj, 1)

            def score(i, s):
                t, h = s // 2, s % 2
                if s == 0:
                    pe.wait_ge(by_act, COPIES * i + 4)
                    pe.wait_ge(by_dve, COPIES * i + 4)
                after(pe, o_lo, 2 * (4 * i + s - 3))
                out = pS[s][:, :].rearrange("p (j b k) -> p j b k", j=4, b=2)
                pe.matmul(pS[s][:, :], identb[:, :], causal[:, :, :], start=True, stop=False, skip_group_check=True)
                for jq in range(4):
                    for b in range(2):
                        tok = slice(P * t + SQ * b, P * t + SQ * b + SQ)
                        for h2 in range(2):
                            rows = slice(E * h2, E * h2 + E)
                            last = pe.matmul(out[rows, jq, b, :], QT[rows, 4 * h + jq, tok], KT[rows, 4 * h + jq, tok],
                                             start=False, stop=True, skip_group_check=True)
                last.then_inc(scored, 1)

            def turn(i, s):
                pe.wait_ge(weighted, 4 * i + s + 1)
                for jq in range(4):
                    last = pe.transpose(pS[s][:, P * jq:P * jq + P], Pr[s][:, jq, :, :].rearrange("p b k -> p (b k)"),
                                        ident[:, :])
                last.then_inc(turned, 1)

            def weigh(i, s):
                t, h = s // 2, s % 2
                pe.wait_ge(pt_done, 4 * i + s + 1)
                if s == 0:
                    pe.wait_ge(by_act, COPIES * (i + 1))
                    pe.wait_ge(by_dve, COPIES * (i + 1))
                after(pe, o_lo, 2 * (4 * i + s - 1))
                apart(pe, waited)
                for jq in range(4):
                    for b in range(2):
                        keys = slice(SQ * b, SQ * b + SQ)
                        for h2 in range(2):
                            head = 2 * (4 * h + jq) + h2
                            last = pe.matmul(o_half(s, b)[E * h2:E * h2 + E, :, :][:, jq, :],
                                             V[keys, t, E * head:E * head + E],
                                             PT[s % 2][keys, jq, SQ * h2:SQ * h2 + SQ], start=True, stop=True)
                last.then_inc(pv_done, 1)

            for k, (kind, part) in enumerate(AHEAD):
                if kind != "X":
                    pe.wait_ge(w_lo, "QK".index(kind) + 1)
                if k >= 2:
                    bank_read(*AHEAD[k - 2], 0)
                fill(k % 2, kind, part, 0)
            pe.wait_ge(w_lo, 4)

            def body(i, last):
                held = [("K", 2, i), ("K", 3, i)] if isinstance(i, int) and i == 0 else [("K", 3, i), ("Y", 1, i - 1)]
                for kind, s, k in plan(last):
                    if kind == "score":
                        score(i, s)
                    elif kind == "turn":
                        turn(i, s)
                    elif kind == "weigh":
                        weigh(i, s)
                    else:
                        quad = i if kind in "VY" else i + 1
                        bank_read(*held[k % 2])
                        held[k % 2] = (kind, s, quad)
                        fill(k % 2, kind, s, quad)

            steps(pe, body)

        def target(kind, part):
            if kind == "Q":
                return QT[:, 2 * part:2 * part + 2, :].rearrange("p j n -> p (j n)")
            if kind == "K":
                return KT[:, 2 * part:2 * part + 2, :].rearrange("p j n -> p (j n)")
            return V[:, part // 2, 512 * (part % 2):512 * (part % 2) + 512]

        def reused(eng, i, kind, part):
            if i is None:
                return
            if kind in "QK":
                eng.wait_ge(scored, 4 * i + 4)
            else:
                after(eng, pv_done, 4 * i)

        @block.scalar
        def _(act):
            def split_w(m):
                act.wait_ge(raw_in[m], 16)
                dst = WO[HI][:, :, :].rearrange("p j d -> p (j d)") if m == 3 else W[m][HI][:, :, :].rearrange(
                    "p k n -> p (k n)")
                act.activation(dst, raw[:, m, :], ACT.Copy).then_inc(w_hi, 1)

            def x_high(r, part, bank):
                act.wait_ge(proj, r + 1)
                act.activation(XT[HI][:, part, :], pJ[bank][:, 0:2 * P], ACT.Copy).then_inc(xt_hi, 1)

            def copy(r, kind, part, bank, i):
                act.wait_ge(proj, r + 1)
                reused(act, i, kind, part)
                act.activation(target(kind, part), pJ[bank][:, :], ACT.Copy).then_inc(by_act, 1)

            def exps(i, s):
                act.wait_ge(shifted, 4 * i + s + 1)
                rows = Pr[s][:, :, :, :].rearrange("p j b k -> p (j b k)")
                act.activation(rows, rows, ACT.Exp, scale=E ** -0.5).then_inc(exped, 1)

            def copy_turned(i, s):
                act.wait_ge(turned, 4 * i + s + 1)
                after(act, pv_done, 4 * i + s - 1)
                act.activation(PT[s % 2][:, :, :].rearrange("p j n -> p (j n)"), pS[s][:, :], ACT.Copy
                               ).then_inc(pt_done, 1)

            def o_high(i, s):
                act.wait_ge(pv_done, 4 * i + s + 1)
                for b in range(2):
                    act.activation(OT[s // 2][HI][:, 4 * (s % 2):4 * (s % 2) + 4, SQ * b:SQ * b + SQ], o_half(s, b),
                                   ACT.Copy).then_inc(o_hi, 1)

            split_w(0)
            for r, (kind, part) in enumerate(AHEAD):
                if r in SPLITS:
                    split_w(SPLITS[r])
                if kind == "X":
                    x_high(r, part, r % 2)
                elif part % 2 == 0:
                    copy(r, kind, part, r % 2, None)

            def body(i, last):
                def fills(kind, part):
                    if kind == "V" or not last:
                        k = place(kind, part, last)
                        if kind == "X":
                            x_high(EV0 + EV * i + k, part, k % 2)
                        else:
                            copy(EV0 + EV * i + k, kind, part, k % 2, i)

                exps(i, 0)
                fills("V", 0)
                exps(i, 1)
                exps(i, 2)
                fills("V", 2)
                exps(i, 3)
                fills("X", 0)
                fills("X", 1)
                copy_turned(i, 0)
                fills("Q", 0)
                copy_turned(i, 1)
                o_high(i, 0)
                fills("Q", 2)
                copy_turned(i, 2)
                o_high(i, 1)
                fills("K", 0)
                copy_turned(i, 3)
                o_high(i, 2)
                fills("K", 2)
                o_high(i, 3)

            steps(act, body)

        @block.vector
        def _(dve):
            def split_w(m):
                dve.wait_ge(w_hi, m + 1)
                high, low = (WO[HI], WO[LO]) if m == 3 else W[m]
                flat = "p j d -> p (j d)"
                dve.tensor_tensor(low[:, :, :].rearrange(flat), raw[:, m, :],
                                  f32(high[:, :, :]).rearrange(flat), ALU.subtract).then_inc(w_lo, 1)

            def statistics(quad):
                statistics_of(dve, stats, mv, X, quad, ln_st, ln_mv, waited)

            def last_norm(quad):
                dve.wait_ge(l3_rs, quad + 1)
                for t in range(2):
                    dve.tensor_scalar(ffn.XN[:, bass.ds(2 * quad + t, 1), :].rearrange("p a d -> p (a d)"),
                                      X[:, bass.ds(2 * quad + t, 1), :].rearrange("p a d -> p (a d)"),
                                      mv3[:, t, 0:1], rstd3[:, t:t + 1], ALU.subtract, ALU.mult).then_inc(l3_xn, 1)
                dve.wait_ge(l3_xn, 2 * quad + 2)
                dve.tensor_reduce(ffn.x_tile_max[:, bass.ds(quad, 1)], ffn.XN[:, bass.ds(2 * quad, 2), :], AX.XY,
                                  ALU.max, apply_absolute_value=True)

            done = 0

            def in_turn(instruction):
                nonlocal done
                done += 1
                instruction.then_inc(made_w, 1)
                dve.wait_ge(made_w, done)

            def normalize(quad):
                dve.wait_ge(ln_rs, quad + 1)
                for t in range(2):
                    dve.tensor_scalar(XN[:, t, :], X[:, bass.ds(2 * quad + t, 1), :].rearrange("p a d -> p (a d)"),
                                      mv[:, t, 0:1], rstd[:, t:t + 1], ALU.subtract, ALU.mult).then_inc(ln_xn, 1)

            def x_low(quad, part, bank):
                dve.wait_ge(xt_hi, 2 * quad + part + 1)
                dve.tensor_tensor(XT[LO][:, part, :], pJ[bank][:, 0:2 * P], f32(XT[HI][:, part, :]), ALU.subtract
                                  ).then_inc(xt_lo, 1)

            def copy(r, kind, part, bank, i):
                dve.wait_ge(proj, r + 1)
                reused(dve, i, kind, part)
                dve.tensor_copy(target(kind, part), pJ[bank][:, :]).then_inc(by_dve, 1)

            def shift(i, s):
                n = 4 * i + s
                dve.wait_ge(scored, n + 1)
                after(dve, shifted, n)
                scores = pS[s][:, :].rearrange("p (j k) -> p j k", k=SQ)
                dve.tensor_reduce(rmax[:, :], scores, AX.X, ALU.max).then_inc(maxed, 1)
                dve.wait_ge(maxed, n + 1)
                dve.tensor_tensor(Pr[s][:, :, :, :].rearrange("p j b k -> p (j b) k"), scores,
                                  rmax[:, :].unsqueeze(2).to_broadcast([P, 8, SQ]), ALU.subtract).then_inc(shifted, 1)

            def sums(i, s):
                dve.wait_ge(exped, 4 * i + s + 1)
                dve.tensor_reduce(rsum[s][:, :], Pr[s][:, :, :, :].rearrange("p j b k -> p (j b) k"), AX.X, ALU.add
                                  ).then_inc(summed, 1)
                dve.wait_ge(summed, 4 * i + s + 1)
                dve.reciprocal(rinv[s][:, :], rsum[s][:, :]).then_inc(inverted, 1)

            def o_low(i, s):
                hs = slice(4 * (s % 2), 4 * (s % 2) + 4)
                for b in range(2):
                    dve.wait_ge(o_hi, 2 * (4 * i + s) + b + 1)
                    toks = slice(SQ * b, SQ * b + SQ)
                    dve.tensor_tensor(OT[s // 2][LO][:, hs, toks], o_half(s, b), f32(OT[s // 2][HI][:, hs, toks]),
                                      ALU.subtract).then_inc(o_lo, 1)

            def add_rows(r, i, t, bank):
                dve.wait_ge(proj, r + 1)
                rows = X[:, bass.ds(2 * i + t, 1), :].rearrange("p a d -> p (a d)")
                dve.tensor_tensor(rows, pJ[bank][:, 0:D], rows, ALU.add).then_inc(x_done, 1)

            def exact_quotient(q, numerator, a):
                r, a_lo, q_lo, left, part = (t[:, :] for t in quotient)
                a_hi, q_hi = (t[:, :] for t in quotient_high)
                in_turn(dve.reciprocal(r, a))
                in_turn(dve.tensor_scalar(q, r, numerator, None, ALU.mult))
                for value, high, low in ((a, a_hi, a_lo), (q, q_hi, q_lo)):
                    in_turn(dve.tensor_copy(high, value))
                    in_turn(dve.tensor_tensor(low, value, f32(high), ALU.subtract))
                in_turn(dve.tensor_tensor(part, f32(q_hi), f32(a_hi), ALU.mult))
                in_turn(dve.tensor_scalar(left, part, -1.0, numerator, ALU.mult, ALU.add))
                for one, other in ((f32(q_hi), a_lo), (q_lo, f32(a_hi)), (q_lo, a_lo)):
                    in_turn(dve.tensor_tensor(part, one, other, ALU.mult))
                    in_turn(dve.tensor_tensor(left, left, part, ALU.subtract))
                in_turn(dve.tensor_tensor(left, left, r, ALU.mult))
                in_turn(dve.tensor_tensor(q, q, left, ALU.add))

            def rows_max(n):
                dve.wait_ge(ffn_in[n], 16)
                in_turn(dve.tensor_reduce(ffn.w_max[:, n, :], raw[:, n, :].rearrange("p (k d) -> p k d", d=D), AX.X,
                                          ALU.max, apply_absolute_value=True))

            def w_scales():
                flat = "p n f -> p (n f)"
                w_max, w_scale = ffn.w_max[:, :, :], ffn.w_scale[:, :, :]
                in_turn(dve.tensor_scalar(w_max, w_max, 1e-8, None, ALU.max))
                exact_quotient(w_scale.rearrange(flat), 127.0, w_max.rearrange(flat))
                in_turn(dve.reciprocal(ffn.w_step[:, :, :], w_scale))

            def round_w(n):
                for f in range(FK):
                    row = raw[:, n, D * f:D * f + D]
                    dve.tensor_scalar(row, row, ffn.w_scale[:, n, f:f + 1], ROUND, ALU.mult, ALU.add
                                      ).then_inc(w_rounded, 1)
                dve.wait_ge(w_rounded, FK * (n + 1))
                ints = (ffn.WI, ffn.WO)[n]
                dve.tensor_scalar(ints[:, :, :].rearrange("p k d -> p (k d)"), raw[:, n, :], -ROUND, None, ALU.add)

            statistics(0)
            normalize(0)
            split_w(0)
            for r, (kind, part) in enumerate(AHEAD):
                if r in SPLITS:
                    split_w(SPLITS[r])
                if kind == "X":
                    x_low(0, part, r % 2)
                elif part % 2:
                    copy(r, kind, part, r % 2, None)

            def body(i, last):
                def fills(kind, part):
                    if kind in "VY" or not last:
                        k = place(kind, part, last)
                        r = EV0 + EV * i + k
                        if kind == "X":
                            x_low(i + 1, part, k % 2)
                        elif kind == "Y":
                            add_rows(r, i, part, k % 2)
                        else:
                            copy(r, kind, part, k % 2, i)

                first = isinstance(i, int) and i == 0
                if not last:
                    statistics(i + 1)
                shift(i, 0)
                shift(i, 1)
                fills("V", 1)
                if not first:
                    statistics_of(dve, stats3, mv3, X, i - 1, l3_st, l3_mv, waited)
                if not last:
                    normalize(i + 1)
                shift(i, 2)
                sums(i, 0)
                shift(i, 3)
                fills("V", 3)
                sums(i, 1)
                fills("X", 0)
                fills("X", 1)
                sums(i, 2)
                sums(i, 3)
                if first:
                    rows_max(0)
                else:
                    last_norm(i - 1)
                fills("Q", 1)
                if first:
                    rows_max(1)
                o_low(i, 0)
                fills("Q", 3)
                if first:
                    w_scales()
                o_low(i, 1)
                fills("K", 1)
                if first:
                    round_w(0)
                fills("Y", 0)
                o_low(i, 2)
                if first:
                    round_w(1)
                o_low(i, 3)
                fills("K", 3)
                fills("Y", 1)

            steps(dve, body)


def feed_forward(nc, X, ident, identb, half, ffn, b_in, b_out, out):
    G = 512
    GROUPS = TOK // G
    GT = G // P
    FK = FF // P
    with ExitStack() as ctx:
        def sb(name, shape, dt):
            return ctx.enter_context(nc.sbuf_tensor("f_" + name, shape, dt))

        def sem(name):
            return ctx.enter_context(nc.semaphore("f_" + name))

        table = sb("table", [P, 1], F32)
        bias_in = sb("bias_in", [P, FK], F32)
        bias_out = sb("bias_out", [P, D], F32)
        WI = sb("WI", [P, KC, FF], BF16)
        stats = sb("stats", [P, 2, 6], F32)
        mv = sb("mv", [P, 2, 2], F32)
        vare = sb("vare", [P, 2], F32)
        rstd = sb("rstd", [P, 2], F32)
        XQ = sb("XQ", [P, GT, D], F32)
        h_tile_max = sb("h_tile_max", [P, FK * GROUPS], F32)
        part_max = [sb(f"part_max_{n}", [P, 1], F32) for n in "xh"]
        all_max = [sb(f"all_max_{n}", [P, 1], F32) for n in "xh"]
        a_max = [sb(f"a_max_{n}", [P, 1], F32) for n in "xh"]
        a_scale = [sb(f"a_scale_{n}", [P, 1], F32) for n in "xh"]
        a_step = [sb(f"a_step_{n}", [P, 1], F32) for n in "xh"]
        h_step = sb("h_step", [P, FK], F32)
        XT = [sb(f"XT{s}", [P, KC, TOK], BF16) for s in "hl"]
        Hid = sb("Hid", [P, FK, TOK], F32)
        RING = FK
        BY_POOL = (3, 7)
        G_parts = [[sb(f"G{r}{s}", [P, G], F32R) for s in "hl"] for r in range(RING)]

        bank = [ctx.enter_context(nc.psum_tensor(f"f_bank{n}", [P, G], F32)) for n in range(7)]
        bankb = ctx.enter_context(nc.psum_tensor("f_bankb", [P, 2 * G], BF16))
        HB = 4

        bi_in, bo_in = sem("bi_in"), sem("bo_in")
        in_turns = sem("in_turns")
        w_turned, w_copied = sem("w_turned"), sem("w_copied")
        waited = sem("waited")
        ln_st, ln_mv, ln_ve, ln_rs, ln_xn = sem("ln_st"), sem("ln_mv"), sem("ln_ve"), sem("ln_rs"), sem("ln_xn")
        x_max, g_max, scaled, biased = sem("x_max"), sem("g_max"), sem("scaled"), sem("biased")
        rounded, x_turned, x_hi, x_lo = sem("rounded"), sem("x_turned"), sem("x_hi"), sem("x_lo")
        first, gelu_done, h_max = sem("first"), sem("gelu"), sem("h_max")
        h_rounded, h_scaled, g_hi, g_lo = sem("h_rounded"), sem("h_scaled"), sem("g_hi"), sem("g_lo")
        g_lo_pool = sem("g_lo_pool")
        second, y_done, stored = sem("second"), sem("y"), sem("stored")

        block = ctx.enter_context(nc.Block())

        def steps(eng, body):
            body(0, False)
            with eng.Fori(1, GROUPS - 1) as g:
                body(g, False)
            body(GROUPS - 1, True)

        def tokens(g):
            return bass.ds(G * g, G)

        def wait_low(eng, g, f):
            if f in BY_POOL:
                eng.wait_ge(g_lo_pool, len(BY_POOL) * g + BY_POOL.index(f) + 1)
            else:
                eng.wait_ge(g_lo, (FK - len(BY_POOL)) * g + f + 1 - sum(q < f for q in BY_POOL))

        def low_part(eng, g, f, done):
            eng.wait_ge(g_hi, FK * g + f + 1)
            eng.tensor_tensor(G_parts[f % RING][LO][:, :], Hid[:, f, tokens(g)], f32(G_parts[f % RING][HI][:, :]),
                              ALU.subtract).then_inc(done, 1)

        @block.sync
        def _(sp):
            sp.dma_start(bias_in[:, :], b_in).then_inc(bi_in, 16)
            sp.dma_start(bias_out[:, :], b_out.partition_broadcast(P)).then_inc(bo_in, 16)

            def body(g, last):
                sp.wait_ge(y_done, GT * g + GT)
                sp.dma_start(out.rearrange("(t p) d -> p t d", p=P)[:, bass.ds(GT * g, GT), :],
                             X[:, bass.ds(GT * g, GT), :]).then_inc(stored, 16)

            steps(sp, body)
            sp.wait_ge(stored, 16 * GROUPS)

        @block.gpsimd
        def _(pool):
            pool.wait_ge(ln_mv, 2)
            pool.tensor_scalar(vare[:, :], mv[:, :, 1], LN_EPS, None, ALU.add).then_inc(ln_ve, 1)
            pool.wait_ge(ln_ve, 1)
            pool.tensor_tensor(rstd[:, :], vare[:, :], half[:, :], ALU.pow).then_inc(ln_rs, 1)
            for n in range(2):
                pool.wait_ge(g_max, 2 * n + 1)
                pool.partition_all_reduce(all_max[n][:, :], part_max[n][:, :], P, RMAX).then_inc(g_max, 1)
                if n == 0:
                    pool.wait_ge(ln_xn, 2)
                    pool.wait_ge(bo_in, 16)
                    for g in range(GROUPS):
                        tiles = X[:, GT * g:GT * g + GT, :]
                        pool.tensor_tensor(tiles, tiles, bias_out[:, :].unsqueeze(1).to_broadcast([P, GT, D]),
                                           ALU.add).then_inc(biased, 1)

            def output(g, last):
                for f in BY_POOL:
                    low_part(pool, g, f, g_lo_pool)

            steps(pool, output)

        @block.tensor
        def _(pe):
            for k in range(KC):
                for f in range(FK):
                    last = pe.transpose(bankb[:, P * f:P * f + P], ffn.WI[:, f, P * k:P * k + P], identb[:, :])
                last.then_inc(w_turned, 1)
                pe.wait_ge(w_copied, k + 1)

            def turn(g):
                pe.wait_ge(rounded, g + 1)
                after(pe, x_lo, 2 * g)
                for k in range(KC):
                    for t in range(GT):
                        last = pe.transpose(bank[HB + k][:, P * t:P * t + P], XQ[:, t, P * k:P * k + P], ident[:, :])
                    last.then_inc(x_turned, 1)

            turn(0)

            def hidden(g, last):
                pe.wait_ge(x_lo, 2 * g + 2)
                for f in range(FK):
                    n = FK * g + f
                    after(pe, gelu_done, n - HB + 1)
                    for k in range(KC):
                        for s in (HI, LO):
                            m = pe.matmul(bank[f % HB][:, :], WI[:, k, P * f:P * f + P], XT[s][:, k, tokens(g)],
                                          start=(k == 0 and s == HI), stop=(k == KC - 1 and s == LO))
                    m.then_inc(first, 1)
                    if f == 1 and not last:
                        turn(g + 1)

            steps(pe, hidden)

            pe.wait_ge(gelu_done, FK * GROUPS)

            def output(g, last):
                for f in range(FK):
                    wait_low(pe, g, f)
                    for t in range(GT):
                        if f == 0:
                            after(pe, y_done, GT * (g - 1) + t + 1)
                        for s in (HI, LO):
                            m = pe.matmul(bank[t][:, 0:D], G_parts[f % RING][s][:, P * t:P * t + P], ffn.WO[:, f, :],
                                          start=(f == 0 and s == HI), stop=(f == FK - 1 and s == LO))
                    m.then_inc(second, 1)

            steps(pe, output)

        @block.scalar
        def _(act):
            act.wait_ge(bi_in, 16)
            act.activation(table[:, :], bias_in[:, 0:1], ACT.Gelu)
            for k in range(KC):
                act.wait_ge(w_turned, k + 1)
                act.activation(WI[:, k, :], bankb[:, :], ACT.Copy).then_inc(w_copied, 1)

            def x_high(g):
                for k in range(KC):
                    act.wait_ge(x_turned, KC * g + k + 1)
                    act.activation(XT[HI][:, k, tokens(g)], bank[HB + k][:, :], ACT.Copy, bias=-ROUND
                                   ).then_inc(x_hi, 1)

            x_high(0)
            act.wait_ge(scaled, 1)

            def hidden(g, last):
                for f in range(FK):
                    act.wait_ge(first, FK * g + f + 1)
                    act.activation(Hid[:, f, tokens(g)], bank[f % HB][:, :], ACT.Gelu, bias=bias_in[:, f:f + 1],
                                   scale=h_step[:, f:f + 1]).then_inc(gelu_done, 1)
                    if f == 2 and not last:
                        x_high(g + 1)

            steps(act, hidden)

            act.wait_ge(gelu_done, FK * GROUPS)
            act.wait_ge(scaled, 2)

            def output(g, last):
                def rounding(g, f):
                    act.activation(Hid[:, f, tokens(g)], Hid[:, f, tokens(g)], ACT.Copy, bias=ROUND,
                                   scale=a_scale[1][:, 0:1]).then_inc(h_rounded, 1)

                if isinstance(g, int) and g == 0:
                    rounding(0, 0)
                for f in range(FK):
                    if f < FK - 1:
                        rounding(g, f + 1)
                    elif not last:
                        rounding(g + 1, 0)
                    n = FK * g + f
                    act.wait_ge(h_scaled, n + 1)
                    after(act, second, n - RING + 1)
                    apart(act, waited)
                    act.activation(G_parts[f % RING][HI][:, :], Hid[:, f, tokens(g)], ACT.Copy).then_inc(g_hi, 1)

            steps(act, output)

        @block.vector
        def _(dve):
            done = 0

            def in_turn(instruction):
                nonlocal done
                done += 1
                instruction.then_inc(in_turns, 1)
                dve.wait_ge(in_turns, done)

            last_tiles = range(TILES - 2, TILES)
            for t, tile_no in enumerate(last_tiles):
                dve.bn_stats(stats[:, t, :], X[:, tile_no, :]).then_inc(ln_st, 1)
            for t in range(2):
                dve.wait_ge(ln_st, t + 1)
                dve.bn_aggr(mv[:, t, :], stats[:, t, :]).then_inc(ln_mv, 1)
            dve.wait_ge(ln_rs, 1)
            for t, tile_no in enumerate(last_tiles):
                dve.tensor_scalar(ffn.XN[:, tile_no, :], X[:, tile_no, :], mv[:, t, 0:1], rstd[:, t:t + 1],
                                  ALU.subtract, ALU.mult).then_inc(ln_xn, 1)
            dve.wait_ge(ln_xn, 2)
            dve.tensor_reduce(ffn.x_tile_max[:, QUADS - 1:QUADS], ffn.XN[:, TILES - 2:TILES, :], AX.XY, ALU.max,
                              apply_absolute_value=True).then_inc(x_max, 1)

            def tile(T, t):
                return T[:, bass.ds(t, 1), :].rearrange("p a d -> p (a d)")

            def scale_of(n, maxima):
                dve.tensor_reduce(part_max[n][:, :], maxima[:, :], AX.X, ALU.max).then_inc(g_max, 1)
                dve.wait_ge(g_max, 2 * n + 2)
                in_turn(dve.tensor_scalar(a_max[n][:, :], all_max[n][:, :], 1e-8, None, ALU.max))
                in_turn(dve.reciprocal(a_step[n][:, :], a_max[n][:, :]))
                in_turn(dve.tensor_scalar(a_scale[n][:, :], a_step[n][:, :], 32767.0, None, ALU.mult))
                in_turn(dve.reciprocal(a_step[n][:, :], a_scale[n][:, :]))

            dve.wait_ge(x_max, 1)
            scale_of(0, ffn.x_tile_max)
            dve.tensor_scalar(h_step[:, :], ffn.w_step[:, 0, :], a_step[0][:, 0:1], None, ALU.mult).then_inc(scaled, 1)

            def rounding(g):
                after(dve, x_turned, KC * g)
                dve.tensor_scalar(XQ[:, :, :], ffn.XN[:, bass.ds(GT * g, GT), :], a_scale[0][:, 0:1], ROUND,
                                  ALU.mult, ALU.add).then_inc(rounded, 1)

            def x_low(g):
                for k in range(KC):
                    dve.wait_ge(x_hi, KC * g + k + 1)
                    dve.scalar_tensor_tensor(XT[LO][:, k, tokens(g)], bank[HB + k][:, :], -ROUND,
                                             XT[HI][:, k, tokens(g)], ALU.add, ALU.subtract).then_inc(x_lo, 1)

            rounding(0)
            x_low(0)

            def hidden(g, last):
                if not last:
                    rounding(g + 1)
                for f in range(FK):
                    n = FK * g + f
                    dve.wait_ge(gelu_done, n + 1)
                    dve.tensor_reduce(h_tile_max[:, bass.ds(n, 1)], Hid[:, f, tokens(g)], AX.X, ALU.max,
                                      apply_absolute_value=True).then_inc(h_max, 1)
                    if f == 2 and not last:
                        x_low(g + 1)

            steps(dve, hidden)
            dve.wait_ge(h_max, FK * GROUPS)
            scale_of(1, h_tile_max)
            dve.sem_inc(scaled, 1)
            dve.wait_ge(biased, GROUPS)

            def add_rows(g, tiles):
                dve.wait_ge(second, FK * g + FK)
                for t in tiles:
                    rows = tile(X, GT * g + t)
                    dve.scalar_tensor_tensor(rows, bank[t][:, 0:D], a_step[1][:, 0:1], rows, ALU.mult, ALU.add
                                             ).then_inc(y_done, 1)

            def output(g, last):
                def weighting(g, f):
                    dve.wait_ge(h_rounded, FK * g + f + 1)
                    dve.tensor_scalar(Hid[:, f, tokens(g)], Hid[:, f, tokens(g)], -ROUND, ffn.w_step[:, 1, f:f + 1],
                                      ALU.add, ALU.mult).then_inc(h_scaled, 1)

                if isinstance(g, int) and g == 0:
                    weighting(0, 0)
                for f in range(FK):
                    if f < FK - 1:
                        weighting(g, f + 1)
                    elif not last:
                        weighting(g + 1, 0)
                    if f not in BY_POOL:
                        low_part(dve, g, f, g_lo)
                    if f in (1, 2) and not (isinstance(g, int) and g == 0):
                        add_rows(g - 1, range(2 * f - 2, 2 * f))
                if last:
                    add_rows(g, range(GT))

            steps(dve, output)


def kernel(x, ctx_1024, mask_B_ik0, L0_xattn_Wq, L0_xattn_Wk, L0_xattn_Wv, L0_xattn_Wo, L0_attn_wq, L0_attn_wk,
           L0_attn_wv, L0_attn_wo, L0_ffn_W_in, L0_ffn_b_in, L0_ffn_W_out, L0_ffn_b_out):
    import numpy as np
    import concourse.bacc as bacc
    from concourse.bass_utils import run_bass_kernel_spmd

    def by_model_width(w):
        return np.asarray(w).reshape(HE, D).T

    laid_out = {
        "x": np.asarray(x).reshape(TOK, D),
        "ctxT": np.asarray(ctx_1024).transpose(2, 0, 1).reshape(D, B * SK),
        "xwq": L0_xattn_Wq, "xwk": L0_xattn_Wk, "xwv": L0_xattn_Wv, "xwo": L0_xattn_Wo,
        "awq": by_model_width(L0_attn_wq), "awk": by_model_width(L0_attn_wk), "awv": by_model_width(L0_attn_wv),
        "awo": np.asarray(L0_attn_wo).T,
        "w_inT": np.asarray(L0_ffn_W_in).T,
        "b_in": np.asarray(L0_ffn_b_in).reshape(FF // P, P).T,
        "w_out": L0_ffn_W_out,
        "b_out": L0_ffn_b_out,
    }
    nc = bacc.Bacc("TRN2", target_bir_lowering=False, num_devices=1)
    arrays, args = {}, {}
    for name, a in laid_out.items():
        arrays[name] = np.ascontiguousarray(a)
        args[name] = nc.dram_tensor(name, arrays[name].shape, F32, kind="ExternalInput").ap()
    out = nc.dram_tensor("out", (TOK, D), F32, kind="ExternalOutput").ap()
    build(nc, **args, out=out)
    result = run_bass_kernel_spmd(nc, [arrays], core_ids=[0])
    return result.results[0]["out"].reshape(B, SQ, D)
```
